# Optimizing a Trainium2 kernel written in Bass

```python
import numpy as np
import jax
import jax.numpy as jnp

def _softmax(x, axis=-1):
    return jax.nn.softmax(x, axis=axis)

def _gelu(x):
    return jax.nn.gelu(x, approximate=True)

def _silu(x):
    return jax.nn.silu(x)

def _sigmoid(x):
    return jax.nn.sigmoid(x)

def _layernorm(x, axis=-1, eps=1e-05):
    m = jnp.mean(x, axis=axis, keepdims=True)
    v = jnp.var(x, axis=axis, keepdims=True)
    return (x - m) / jnp.sqrt(v + eps)

def _scatter_add(tgt, idx, src, axis=0):
    return tgt.at[idx].add(src)

def _segment_sum(src, seg, n):
    return jax.ops.segment_sum(src, seg, n)
kernel_name = 'mk_seq_preln_d1_jaxref_r8_a0a3b4'

def setup_inputs(seed: int=0):
    np.random.seed(seed)
    _w = jnp.asarray

    def _L0_attn_setup():
        import jax, jax.numpy as jnp
        import numpy as np
        B, S, D = (2, 512, 256)
        H, DK, DV = (16, 128, 128)
        SEG = 64
        UPDATE = 'delta'
        CAUSAL = True
        key = jax.random.key(seed)
        ks = jax.random.split(key, 6)
        s = 0.02
        return {'x': jax.random.normal(ks[0], (B, S, D), jnp.float32), 'Wq': jax.random.normal(ks[1], (D, H * DK), jnp.float32) * s, 'Wk': jax.random.normal(ks[2], (D, H * DK), jnp.float32) * s, 'Wv': jax.random.normal(ks[3], (D, H * DV), jnp.float32) * s, 'Wo': jax.random.normal(ks[4], (H * DV, D), jnp.float32) * s, 'betas': jax.random.normal(ks[5], (1, H, 1, DV), jnp.float32)}
    _L0_attn_in = _L0_attn_setup()

    def _L0_ffn_setup():
        import jax, jax.numpy as jnp
        import numpy as np
        B, S, H, I, E, K = (4, 256, 256, 512, 8, 2)
        key = jax.random.key(seed)
        k1, k2, k3, k4 = jax.random.split(key, 4)
        return {'hidden_states': jax.random.normal(k1, (B, S, H), dtype=jnp.float32), 'gate_weight': jax.random.normal(k2, (E, H), dtype=jnp.float32) * 0.02, 'gate_up_proj': jax.random.normal(k3, (E, 2 * I, H), dtype=jnp.float32) * 0.02, 'down_proj': jax.random.normal(k4, (E, H, I), dtype=jnp.float32) * 0.02}
    _L0_ffn_in = _L0_ffn_setup()
    _d = {'L0_attn_x': _L0_attn_in['x'], 'L0_attn_Wq': _L0_attn_in['Wq'], 'L0_attn_Wk': _L0_attn_in['Wk'], 'L0_attn_Wv': _L0_attn_in['Wv'], 'L0_attn_Wo': _L0_attn_in['Wo'], 'L0_attn_betas': _L0_attn_in['betas'], 'L0_ffn_gate_weight': _L0_ffn_in['gate_weight'], 'L0_ffn_gate_up_proj': _L0_ffn_in['gate_up_proj'], 'L0_ffn_down_proj': _L0_ffn_in['down_proj']}
    _x0 = _d['L0_attn_x']
    _d['L0_attn_x'] = jax.random.normal(jax.random.fold_in(jax.random.key(seed), 1), (8, 256, 256), dtype=_x0.dtype)
    del _x0
    return _d

def reference(L0_attn_x, L0_attn_Wq, L0_attn_Wk, L0_attn_Wv, L0_attn_Wo, L0_attn_betas, L0_ffn_gate_weight, L0_ffn_gate_up_proj, L0_ffn_down_proj):

    def _L0_attn_ref(x, Wq, Wk, Wv, Wo, betas):
        import jax, jax.numpy as jnp
        import numpy as np
        B, S, D = (2, 512, 256)
        H, DK, DV = (16, 128, 128)
        SEG = 64
        UPDATE = 'delta'
        CAUSAL = True
        Bsz, seq, _ = x.shape
        nseg = seq // SEG
        q = (x @ Wq).reshape(Bsz, seq, H, DK).transpose(0, 2, 1, 3)
        k = (x @ Wk).reshape(Bsz, seq, H, DK).transpose(0, 2, 1, 3)
        v = (x @ Wv).reshape(Bsz, seq, H, DV).transpose(0, 2, 1, 3)
        qs = q.reshape(Bsz, H, nseg, SEG, DK).transpose(2, 0, 1, 3, 4)
        ks_ = k.reshape(Bsz, H, nseg, SEG, DK).transpose(2, 0, 1, 3, 4)
        vs = v.reshape(Bsz, H, nseg, SEG, DV).transpose(2, 0, 1, 3, 4)
        causal_mask = jnp.tril(jnp.ones((SEG, SEG), bool))
        scale = DK ** 0.5
        beta = jax.nn.sigmoid(betas)

        def step(carry, seg):
            mem, z = carry
            qq, kk, vv = seg
            sigma_q = jax.nn.elu(qq) + 1.0
            scores = jnp.einsum('bhsk,bhtk->bhst', qq, kk) / scale
            if CAUSAL:
                scores = jnp.where(causal_mask, scores, -jnp.inf)
            att_dot = jax.nn.softmax(scores, axis=-1) @ vv
            att_mem = sigma_q @ mem / (sigma_q @ z)
            sigma_k = jax.nn.elu(kk) + 1.0
            if UPDATE == 'linear':
                mem_new = mem + jnp.einsum('bhsk,bhsv->bhkv', sigma_k, vv)
            else:
                delta = vv - sigma_k @ mem / (sigma_k @ z)
                mem_new = mem + jnp.einsum('bhsk,bhsv->bhkv', sigma_k, delta)
            z_new = z + sigma_k.sum(axis=-2, keepdims=True).transpose(0, 1, 3, 2)
            att = beta * att_mem + (1.0 - beta) * att_dot
            out = att.reshape(Bsz, SEG, H * DV) @ Wo
            return ((mem_new, z_new), out)
        mem0 = jnp.zeros((Bsz, H, DK, DV), x.dtype)
        z0 = jnp.ones((Bsz, H, DK, 1), x.dtype) / DK
        _, outs = jax.lax.scan(step, (mem0, z0), (qs, ks_, vs))
        return outs.transpose(1, 0, 2, 3).reshape(Bsz, seq, D)

    def _L0_ffn_ref(hidden_states, gate_weight, gate_up_proj, down_proj):
        import jax, jax.numpy as jnp
        import numpy as np
        B, S, H, I, E, K = (4, 256, 256, 512, 8, 2)
        b, s, h = hidden_states.shape
        num_experts, top_k = (gate_weight.shape[0], K)
        x = hidden_states.reshape(-1, h)
        router_logits = x @ gate_weight.T
        probs = jax.nn.softmax(router_logits.astype(jnp.float32), axis=-1)
        top_v, top_i = jax.lax.top_k(probs, top_k)
        top_v = top_v / top_v.sum(axis=-1, keepdims=True)
        combine_w = jnp.einsum('tke,tk->te', jax.nn.one_hot(top_i, num_experts, dtype=top_v.dtype), top_v).astype(x.dtype)

        def expert_step(acc, inp):
            gu, dp, w = inp
            gate, up = jnp.split(x @ gu.T, 2, axis=-1)
            hidden = jax.nn.silu(gate) * up
            y = hidden @ dp.T
            return (acc + w[:, None] * y, None)
        out, _ = jax.lax.scan(expert_step, jnp.zeros_like(x), (gate_up_proj, down_proj, combine_w.T))
        return out.reshape(b, s, h)
    x = L0_attn_x
    x = x + _L0_attn_ref(_layernorm(x, axis=-1), L0_attn_Wq, L0_attn_Wk, L0_attn_Wv, L0_attn_Wo, L0_attn_betas)
    x = x + _L0_ffn_ref(_layernorm(x, axis=-1), L0_ffn_gate_weight, L0_ffn_gate_up_proj, L0_ffn_down_proj)
    return x

_drawn_inputs = setup_inputs


def setup_inputs(seed=0):
    import zlib

    import numpy as np

    out = dict(_drawn_inputs(seed))
    spreads = {}
    factors = {'L0_attn_Wq': 8.0,
     'L0_attn_Wk': 8.0,
     'L0_attn_betas': 3.197,
     'L0_ffn_gate_weight': 3.802,
     'L0_ffn_gate_up_proj': 3.306,
     'L0_ffn_down_proj': 3.31}
    for name, (base, spread) in spreads.items():
        noise = np.random.default_rng([zlib.crc32(name.encode()), seed]).standard_normal(out[name].shape)
        drawn = base * np.exp(spread * noise) if base else spread * noise
        out[name] = jnp.asarray(drawn.astype(out[name].dtype))
    for name, factor in factors.items():
        out[name] = (out[name] * factor).astype(out[name].dtype)
    return out
```

```python
from contextlib import ExitStack

import numpy as np
import concourse.bass as bass
import concourse.mybir as mybir

F32 = mybir.dt.float32
F32R = mybir.dt.float32r
BF16 = mybir.dt.bfloat16
I32 = mybir.dt.int32
U32 = mybir.dt.uint32
ALU = mybir.AluOpType
ACT = mybir.ActivationFunctionType
AX_X = mybir.AxisListType.X

P = 128
BATCH, SEQ, D = 8, 256, 256
HEADS, DK, SEG = 16, 128, 64
NSEG = SEQ // SEG
PAIRS = HEADS // 2
UNITS = BATCH * PAIRS
TILES = BATCH * SEQ // P
KC = D // P
PW = 2 * P
VW = DK + 1
EPS = 1e-5
MASKED = -1e30
EXPERTS, INNER = 8, 512
IC = INNER // P
STEPS_DVE, STEPS_POOL = 5, 12
SLOTS = (2 * BATCH * SEQ // P + EXPERTS) * P
ROW = D + 2
NO_TOKEN = 1 << 30
MADE = 8
RSQRT_GUESS = float(0x5F3759DF)


class Norm:

    def __init__(self, sb, sem, name, tiles):
        self.stats = sb(f"{name}_stats", [P, tiles, 6])
        self.mv = sb(f"{name}_mv", [P, tiles, 2])
        self.v = sb(f"{name}_v", [P, tiles])
        self.y = sb(f"{name}_y", [P, tiles])
        self.t = sb(f"{name}_t", [P, tiles])
        self.stats_done = sem(f"{name}_stats_done")
        self.guess = sem(f"{name}_guess")
        self.newton = sem(f"{name}_newton")
        self.tiles = tiles


def attention(nc, x_ln, x_res, Wqkv, Wo, betas, gate, logits, x2_out, xn2_out, slot_rows):
    ctx = ExitStack()
    with ctx:
        def sb(name, shape, dt=F32):
            return ctx.enter_context(nc.sbuf_tensor(name, shape, dt))

        def bank(name):
            return ctx.enter_context(nc.psum_tensor(name, [P, 512], F32))

        def sem(name):
            return ctx.enter_context(nc.semaphore(name))

        ident = sb("ident", [P, P])
        causal = sb("causal", [P, SEG])
        three_halves = sb("three_halves", [P, 2])
        z_start = sb("z_start", [P, 2, VW])
        beta = sb("beta", [P, HEADS, DK])
        beta_rest = sb("beta_rest", [P, HEADS, DK])
        w_hi = sb("w_hi", [P, PAIRS, 3, KC, PW], F32R)
        w_lo = sb("w_lo", [P, PAIRS, 3, KC, PW], F32R)
        wo = sb("wo", [P, HEADS, D])
        w_stage = sb("w_stage", [P, 3, KC, PW])
        x_in = sb("x_in", [P, 2, D])
        xn = sb("xn", [P, 2, D])
        xT_hi = sb("xT_hi", [P, KC, SEQ], F32R)
        xT_lo = sb("xT_lo", [P, KC, SEQ], F32R)
        xr = sb("xr", [P, D])
        x2 = sb("x2", [P, D])
        xn2 = sb("xn2", [P, D])
        xn2T = sb("xn2T", [P, KC, P])
        gate_sb = sb("gate_sb", [P, KC, EXPERTS])
        empty = sb("empty", [P, ROW])
        qk = sb("qk", [P, 2, 512])
        ex = sb("ex", [P, 2, 448])
        sig = sb("sig", [P, 2, 2, 448])
        v1 = sb("v1", [P, 2, 2, 2, VW])
        sk = sb("sk", [P, 2, 2, DK])
        mem = sb("mem", [P, 2, VW])
        delta = sb("delta", [P, 2, VW])
        rz = sb("rz", [P, 3, 2])
        sm = sb("sm", [P, 4, SEG])
        mx = sb("mx", [P, 4])
        pr = sb("pr", [P, 4, P])
        prT = sb("prT", [P, 4, P])
        rs = sb("rs", [P, 4])
        rr = sb("rr", [P, 4])
        att = sb("att", [P, 2, 2, DK])
        attm = sb("attm", [P, 2, 2, DK])
        aT = sb("aT", [P, 2, HEADS, P])

        QK = [bank("QK0"), bank("QK1")]
        TA, TB, TC, MEM, MO, OUT = (bank(n) for n in ("TA", "TB", "TC", "MEM", "MO", "OUT"))
        mem_ps = MEM[:, 0:2 * VW].rearrange("p (h n) -> p h n", h=2)
        mo = MO[:, 0:2 * VW].rearrange("p (h n) -> p h n", h=2)

        consts = sem("consts")
        const_dma = sem("const_dma")
        beta_ready = sem("beta_ready")
        stage_in = sem("stage_in")
        wo_dma = sem("wo_dma")
        w_hi_done = sem("w_hi_done")
        w_lo_done = sem("w_lo_done")
        x_in_dma, xr_dma, x2_dma = sem("x_in_dma"), sem("xr_dma"), sem("x2_dma")
        ln1, ln2 = Norm(sb, sem, "ln1", 2), Norm(sb, sem, "ln2", 1)
        empty_done, slots_dma, gate_dma, xn2_dma = sem("empty_done"), sem("slots_dma"), sem("gate_dma"), sem("xn2_dma")
        xn2_done, xn2t, xn2T_done, lg, lg_done = (sem(n) for n in ("xn2_done", "xn2t", "xn2T_done", "lg", "lg_done"))
        xn_done, xt_done, xT_hi_done, xT_lo_done = (sem(n) for n in ("xn_done", "xt_done", "xT_hi_done", "xT_lo_done"))
        skt, sc, sm1, sm2, sm3, upd0, upd1, upd2, vp, pt, pv, attt, op = (sem(n) for n in (
            "skt", "sc", "sm1", "sm2", "sm3", "upd0", "upd1", "upd2", "vp", "pt", "pv", "attt", "op"))
        proj = [sem("projA"), sem("projB")]
        qkc = [sem("qkcA"), sem("qkcB")]
        exd = [sem("exA"), sem("exB")]
        mind = [sem("minA"), sem("minB")]
        sigd = [sem("sigA"), sem("sigB")]
        sk_done, v_done, prT_done, aT_done = (sem(n) for n in ("sk_done", "v_done", "prT_done", "aT_done"))
        masked, mx_done, sub_done, pr_done, sum_done, rr_done = (sem(n) for n in ("masked", "mx_done", "sub_done", "pr_done", "sum_done", "rr_done"))
        mem_done = [sem(f"mem_done{i}") for i in (1, 2, 3)]
        rz_done = [sem(f"rz_done{i}") for i in (1, 2, 3)]
        delta_done = [sem(f"delta_done{i}") for i in (1, 2)]
        attm_done = [sem(f"attm_done{i}") for i in (1, 2, 3)]
        dot_done, dotb_done, att_done = sem("dot_done"), sem("dotb_done"), sem("att_done")
        x2_done = sem("x2_done")
        ln_c, causal_done = sem("ln_c"), sem("causal_done")

        def has(eng, s, unit, each=1):
            if isinstance(unit, int) and unit < 0:
                return
            eng.wait_ge(s, (unit + 1) * each)

        block = ctx.enter_context(nc.Block())

        def out_half(b, g):
            return None if b is None or (isinstance(b, int) and 2 * b + g // 4 < 1) else 2 * b + g // 4 - 1

        def routed_half(b, g):
            return None if b is None or (isinstance(b, int) and b < 1) else 2 * b + g // 4 - 2

        def last_routed(b, g):
            if g % 4 or b is None or (isinstance(b, int) and 2 * b + g // 4 < 3):
                return None
            return 2 * b + g // 4 - 3

        def run_slots(engine, slot):
            slot(None, -1, PAIRS - 1, False, True, False)
            for g in range(PAIRS):
                slot(0, g, g, True, True, g > 0)
            with engine.Fori(1, BATCH - 1) as b:
                for g in range(PAIRS):
                    slot(b, b * PAIRS + g, g, True, True, True)
            for g in range(PAIRS):
                slot(BATCH - 1, (BATCH - 1) * PAIRS + g, g, True, g < PAIRS - 1, True)
            slot(BATCH, UNITS, 0, False, False, True)

        @block.sync
        def _(sp):
            def stage(g):
                has(sp, w_lo_done, g - 1)
                sp.dma_start(w_stage[:], Wqkv[g]).then_inc(stage_in, 16)

            def store_xn2(n):
                has(sp, xn2_done, n)
                sp.dma_start(xn2_out[n], xn2[:]).then_inc(xn2_dma, 16)

            def load_x_in(b):
                has(sp, xn_done, b - 1)
                sp.dma_start(x_in[:], x_ln[b]).then_inc(x_in_dma, 16)

            def slot(b, u, g, cur, nxt, prv):
                if b is None:
                    load_x_in(0)
                    stage(0)
                    sp.dma_start(beta[:], betas.partition_broadcast(P)).then_inc(const_dma, 16)
                    stage(1)
                    sp.dma_start(wo[:], Wo).then_inc(wo_dma, 16)
                    sp.dma_start(gate_sb[:], gate).then_inc(gate_dma, 16)
                    sp.wait_ge(empty_done, 2)
                    sp.dma_start(slot_rows.rearrange("(n p) r -> p n r", p=P), empty[:, None, :].broadcast_to([P, SLOTS // P, ROW]))\
                      .then_inc(slots_dma, 16)
                if b is not None and isinstance(u, int) and u + 2 < PAIRS:
                    stage(u + 2)
                if g == 1 and cur and not (isinstance(b, int) and b == BATCH - 1):
                    load_x_in(b + 1)
                half, routed = out_half(b, g), routed_half(b, g)
                if half is None:
                    return
                if routed is not None and g % 4 == 2:
                    store_xn2(routed)
                if g % 4 == 0:
                    has(sp, x2_done, half - 1)
                    sp.dma_start(xr[:], x_res[half]).then_inc(xr_dma, 16)
                if not cur:
                    store_xn2(TILES - 2)
                if g % 4 == 3 or not cur:
                    has(sp, x2_done, half)
                    sp.dma_start(x2_out[half], x2[:]).then_inc(x2_dma, 16)
                if not cur:
                    store_xn2(TILES - 1)

            run_slots(sp, slot)
            sp.wait_ge(x2_dma, 16 * TILES)
            sp.wait_ge(xn2_dma, 16 * TILES)
            sp.wait_ge(slots_dma, 16)

        @block.tensor
        def _(pe):
            def exact(out, a_hi, a_lo, b_hi, b_lo, first, last, **kw):
                pe.matmul(out, a_hi, b_lo, start=first, stop=False, **kw)
                pe.matmul(out, a_hi, b_hi, start=False, stop=False, **kw)
                return pe.matmul(out, a_lo, b_hi, start=False, stop=last, **kw)

            def transpose_x(b):
                has(pe, xn_done, b)
                has(pe, exd[1], b * PAIRS - 1)
                has(pe, qkc[1], b * PAIRS - 1)
                for t in range(2):
                    for c in range(KC):
                        m = pe.transpose(QK[1][:, (2 * c + t) * P:(2 * c + t + 1) * P], xn[:, t, c * P:(c + 1) * P], ident[:])
                m.then_inc(xt_done, 1)

            def turn_xn2(n, u):
                has(pe, xn2_done, n)
                has(pe, exd[1], u + 1)
                has(pe, qkc[1], u + 1)
                for c in range(KC):
                    m = pe.transpose(QK[1][:, c * P:(c + 1) * P], xn2[:, c * P:(c + 1) * P], ident[:])
                m.then_inc(xn2t, 1)

            def route(n):
                has(pe, xn2T_done, n)
                for c in range(KC):
                    m = pe.matmul(QK[1][:, 0:EXPERTS], xn2T[:, c], gate_sb[:, c], start=c == 0, stop=c == KC - 1)
                m.then_inc(lg, 1)

            def project(h, u, gn, b, routed=None):
                if h == 0:
                    has(pe, w_lo_done, gn if isinstance(u, int) and u < PAIRS else PAIRS - 1)
                    has(pe, xT_lo_done, b)
                has(pe, exd[h], u - 1)
                has(pe, qkc[h], u - 1)
                if h == 1 and gn == 0:
                    has(pe, xT_lo_done, b)
                if h == 1 and routed is not None:
                    has(pe, lg_done, routed)
                blocks = QK[h][:, :].rearrange("p (s m t) -> p m s t", m=2, t=SEG)
                for m in range(2):
                    for c in range(KC):
                        a = slice(h * P, (h + 1) * P)
                        mm = exact(blocks[:, m], w_hi[:, gn, m, c, a], w_lo[:, gn, m, c, a],
                                   xT_hi[:, c, :], xT_lo[:, c, :], c == 0, c == KC - 1)
                mm.then_inc(proj[h], 1)

            def project_v(u, gn):
                has(pe, sk_done, u - 1)
                for t in range(2):
                    for c in range(KC):
                        a = slice(t * P, (t + 1) * P)
                        mm = exact(TA[:, t * PW:(t + 1) * PW], xT_hi[:, c, a], xT_lo[:, c, a],
                                   w_hi[:, gn, 2, c, :], w_lo[:, gn, 2, c, :], c == 0, c == KC - 1)
                mm.then_inc(vp, 1)

            def sk_rows(u, par):
                has(pe, v_done, u)
                has(pe, sigd[1], u)
                for h in range(2):
                    s = sig[:, par, h]
                    pe.transpose(TA[:, (2 * h) * P:(2 * h + 1) * P], s[:, 64:192], ident[:])
                    pe.transpose(TA[0:SEG, (2 * h) * P:(2 * h + 1) * P], s[:, 0:64], ident[:])
                    m = pe.transpose(TA[:, (2 * h + 1) * P:(2 * h + 2) * P], s[:, 320:448], ident[:])
                m.then_inc(skt, 1)

            def scores(u):
                has(pe, prT_done, u - 1)
                for h in range(2):
                    for s, (blk, row, t) in enumerate(((0, 64, 0), (1, 0, 0), (3, 0, 1), (2, 64, 1))):
                        q = qk[:, h, blk * 128:blk * 128 + SEG]
                        k = qk[:, h, blk * 128 + SEG:blk * 128 + 2 * SEG]
                        o = (2 * h + t) * SEG
                        m = pe.matmul(TB[row:row + SEG, o:o + SEG], q, k, start=True, stop=True)
                m.then_inc(sc, 1)

            def update(step, u, par):
                if step == 0:
                    has(pe, sk_done, u)
                    has(pe, mem_done[2], u - 1)
                else:
                    has(pe, delta_done[step - 1], u)
                rows = slice(0, SEG) if step == 0 else slice(SEG, P)
                for h in range(2):
                    d = v1[rows, par, 0, h] if step == 0 else delta[rows, h]
                    m = pe.matmul(mem_ps[:, h], sk[rows, h, step // 2], d, start=(step == 0 and h == 0),
                                  stop=(step == 2), skip_group_check=True)
                m.then_inc((upd0, upd1, upd2)[step], 1)

            def read_memory(step, u, par):
                has(pe, mem_done[step - 1], u)
                if step == 1:
                    has(pe, attm_done[2], u - 1)
                else:
                    has(pe, attm_done[step - 2], u)
                for h in range(2):
                    s = sig[:, par, h]
                    if step == 3:
                        m = pe.matmul(mo[SEG:P, h], s[:, 192:256], mem[:, h], start=True, stop=True)
                    else:
                        o = 64 if step == 1 else 320
                        m = pe.matmul(mo[:, h], s[:, o:o + P], mem[:, h], start=True, stop=True)
                m.then_inc((sm1, sm2, sm3)[step - 1], 1)

            def turn_att(u):
                has(pe, att_done, u)
                for h in range(2):
                    for t in range(2):
                        o = (2 * h + t) * P
                        m = pe.transpose(TC[:, o:o + P], att[:, h, t], ident[:])
                m.then_inc(attt, 1)

            def turn_probs(u):
                has(pe, pr_done, u)
                for j in range(4):
                    m = pe.transpose(TB[:, j * P:(j + 1) * P], pr[:, j], ident[:])
                m.then_inc(pt, 1)

            def probs_v(u, par):
                has(pe, prT_done, u)
                has(pe, aT_done, u - 1)
                for h in range(2):
                    for t in range(2):
                        o = (2 * h + t) * P
                        m = pe.matmul(TC[:, o:o + P], prT[:, 2 * h + t], v1[:, par, t, h, 0:DK], start=True, stop=True)
                m.then_inc(pv, 1)

            def project_out(part, u, half, g, steps):
                if isinstance(half, int) and half == 0 and g == 4:
                    pe.wait_ge(wo_dma, 16)
                if part == 0 and g % 4 == 0:
                    has(pe, aT_done, u)
                    has(pe, x2_done, half - 1)
                for m in steps:
                    mm = pe.matmul(OUT[:, 0:D], aT[:, (g // 4 + 1) % 2, m], wo[:, m], start=m == 0, stop=m == HEADS - 1)
                    if m == HEADS - 1:
                        mm.then_inc(op, 1)

            def slot(b, u, g, cur, nxt, prv):
                par, gn = g % 2, (g + 1) % PAIRS
                if b is None:
                    pe.wait_ge(consts, 8)
                    pe.wait_ge(gate_dma, 16)
                    transpose_x(0)
                bn = 0 if b is None else (b + 1 if g == PAIRS - 1 else b)
                half = out_half(b, g)
                steps = range(g % 4 * 4, g % 4 * 4 + 4) if cur else range(HEADS)
                if cur:
                    sk_rows(u, par)
                    scores(u)
                if prv:
                    read_memory(3, u - 1, 1 - par)
                if nxt:
                    project(0, u + 1, gn, bn)
                if cur:
                    update(0, u, par)
                if nxt:
                    project(1, u + 1, gn, bn, last_routed(b, g))
                if cur:
                    read_memory(1, u, par)
                if prv:
                    turn_att(u - 1)
                if nxt:
                    project_v(u + 1, gn)
                if cur:
                    update(1, u, par)
                    turn_probs(u)
                routed = routed_half(b, g)
                if cur and routed is not None and g % 4 == 3:
                    turn_xn2(routed, u if nxt else u - 1)
                if half is not None:
                    project_out(0, u - 1, half, g, steps[:len(steps) // 2])
                if cur:
                    read_memory(2, u, par)
                    probs_v(u, par)
                if g == PAIRS - 2 and cur and not (isinstance(b, int) and b == BATCH - 1):
                    transpose_x(b + 1)
                if half is not None:
                    project_out(1, u - 1, half, g, steps[len(steps) // 2:])
                if cur and routed is not None and g % 4 == 3:
                    route(routed)
                if b is not None and not cur:
                    for n in (TILES - 2, TILES - 1):
                        has(pe, lg_done, n - 1)
                        turn_xn2(n, UNITS - 2)
                        route(n)
                if cur:
                    update(2, u, par)

            run_slots(pe, slot)

        @block.scalar
        def _(act):
            def split_hi(g):
                act.wait_ge(stage_in, 16 * (g + 1))
                act.activation(w_hi[:, g], w_stage[:], ACT.Copy).then_inc(w_hi_done, 1)

            def slot(b, u, g, cur, nxt, prv):
                par = g % 2
                if b is None:
                    act.wait_ge(const_dma, 16)
                    act.activation(beta[:], beta[:], ACT.Sigmoid).then_inc(beta_ready, 1)
                    split_hi(0)
                    turn_x_hi(0)
                    split_hi(1)
                if cur:
                    has(act, skt, u)
                    act.activation(sk[:], TA[:, :], ACT.Copy).then_inc(sk_done, 1)
                for h in range(2):
                    if nxt:
                        has(act, proj[h], u + 1)
                        act.activation(qk[:, h], QK[h][:, :], ACT.Copy).then_inc(qkc[h], 1)
                        act.activation(ex[:, h], QK[h][:, 64:512], ACT.Exp).then_inc(exd[h], 1)
                    if h == 0 and cur:
                        has(act, sub_done, u)
                        for rows, cols in ((slice(0, SEG), slice(SEG, P)), (slice(SEG, P), slice(0, SEG))):
                            m = act.activation(pr[rows, :, cols], sm[rows], ACT.Exp, scale=float(DK) ** -0.5)
                        m.then_inc(pr_done, 1)
                if prv:
                    has(act, attt, u - 1)
                    gp = (g - 1) % PAIRS
                    for h in range(2):
                        row = (2 * gp + h) % PAIRS * 4
                        m = act.activation(aT[:, gp // 4, :, :].rearrange("p m (s r) -> p s r m", s=NSEG)[:, :, row:row + 4],
                                           TC[:, h * SEQ:(h + 1) * SEQ].rearrange("p (s i m) -> p s i m", s=NSEG, i=4), ACT.Copy)
                    m.then_inc(aT_done, 1)
                if nxt:
                    has(act, vp, u + 1)
                    act.activation(v1[:, 1 - par, :, :, 0:DK], TA[:, :].rearrange("p (t h n) -> p t h n", t=2, h=2),
                                   ACT.Copy).then_inc(v_done, 1)
                if cur:
                    has(act, pt, u)
                    act.activation(prT[:], TB[:, :], ACT.Copy).then_inc(prT_done, 1)
                    if routed_half(b, g) is not None and g % 4 == 3:
                        keep_xn2T(routed_half(b, g))
                    has(act, pv, u)
                    has(act, rr_done, u)
                    for h in range(2):
                        for t in range(2):
                            j = 2 * h + t
                            m = act.activation(att[:, h, t], TC[:, j * P:(j + 1) * P], ACT.Copy, scale=rr[:, j:j + 1])
                    m.then_inc(dot_done, 1)
                if g == PAIRS - 2 and cur and not (isinstance(b, int) and b == BATCH - 1):
                    turn_x_hi(b + 1)
                if b is not None and not cur:
                    keep_xn2T(TILES - 2)
                    keep_xn2T(TILES - 1)
                if b is not None and isinstance(u, int) and u + 2 < PAIRS:
                    split_hi(u + 2)

            def keep_xn2T(n):
                has(act, xn2t, n)
                act.activation(xn2T[:], QK[1][:, 0:KC * P], ACT.Copy).then_inc(xn2T_done, 1)

            def turn_x_hi(b):
                has(act, xt_done, b)
                act.activation(xT_hi[:], QK[1][:, :], ACT.Copy).then_inc(xT_hi_done, 1)

            run_slots(act, slot)

        @block.vector
        def _(dve):
            def split_lo(g):
                has(dve, w_hi_done, g)
                dve.tensor_tensor(w_lo[:, g], w_stage[:], w_hi[:, g], ALU.subtract).then_inc(w_lo_done, 1)

            def norm_stats(ln, src):
                for t in range(ln.tiles):
                    dve.bn_stats(ln.stats[:, t], src[t]).then_inc(ln.stats_done, 1)

            def norm_guess(ln, n):
                def step(ins, k):
                    ins.then_inc(ln.guess, 1)
                    dve.wait_ge(ln.guess, n * STEPS_DVE + k)

                for t in range(ln.tiles):
                    m = dve.bn_aggr(ln.mv[:, t], ln.stats[:, t])
                step(m, 1)
                step(dve.tensor_scalar(ln.v[:], ln.mv[:, :, 1], EPS, None, ALU.add), 2)
                step(dve.tensor_scalar(ln.y[:].bitcast(I32), ln.v[:].bitcast(I32), 1, None, ALU.logical_shift_right), 3)
                dve.tensor_scalar(ln.y[:].bitcast(I32), ln.y[:].bitcast(I32), -1.0, RSQRT_GUESS, ALU.mult, ALU.add).then_inc(ln.guess, 1)
                dve.tensor_scalar(ln.v[:], ln.v[:], -0.5, None, ALU.mult).then_inc(ln.guess, 1)

            def normalise(ln, n, src, dst, done):
                has(dve, ln.newton, n, STEPS_POOL)
                for t in range(ln.tiles):
                    m = dve.tensor_scalar(dst[t], src[t], ln.mv[:, t, 0:1], ln.y[:, t:t + 1], ALU.subtract, ALU.mult)
                m.then_inc(done, 1)

            x_in_t, xn_t = [x_in[:, t] for t in range(2)], [xn[:, t] for t in range(2)]

            def normalise_x2(n):
                normalise(ln2, n, [x2[:]], [xn2[:]], xn2_done)

            def keep_logits(n):
                has(dve, xn2_dma, n, 16)
                has(dve, lg, n)
                dve.tensor_scalar(logits[:, n, :], QK[1][:, 0:EXPERTS], 1.0, None, ALU.mult).then_inc(lg_done, 1)

            def residual(half):
                has(dve, op, half)
                has(dve, xr_dma, half, 16)
                has(dve, x2_dma, half - 1, 16)
                dve.tensor_tensor(x2[:], OUT[:, 0:D], xr[:], ALU.add).then_inc(x2_done, 1)

            def turn_x_lo(b):
                has(dve, xT_hi_done, b)
                dve.tensor_tensor(xT_lo[:], QK[1][:, :], xT_hi[:], ALU.subtract).then_inc(xT_lo_done, 1)

            def sigma(h, u, par):
                has(dve, exd[h], u)
                dve.tensor_scalar(ex[:, h], ex[:, h], 1.0, None, ALU.min).then_inc(mind[h], 1)
                has(dve, mind[h], u)
                dve.scalar_tensor_tensor(sig[:, par, h], qk[:, h, 64:512], 0.0, ex[:, h], ALU.max, ALU.add).then_inc(sigd[h], 1)

            def copy_memory(step, u):
                has(dve, (upd0, upd1, upd2)[step - 1], u)
                dve.tensor_tensor(mem[:], mem_ps, z_start[:], ALU.add).then_inc(mem_done[step - 1], 1)

            def use_memory(step, u, par):
                g_beta = beta_of
                rows = {1: slice(0, P), 2: slice(0, P), 3: slice(SEG, P)}[step]
                has(dve, (sm1, sm2, sm3)[step - 1], u)
                dve.reciprocal(rz[rows, step - 1], mo[rows, :, DK]).then_inc(rz_done[step - 1], 1)
                has(dve, rz_done[step - 1], u)
                if step < 3:
                    for h in range(2):
                        r = slice(SEG, P)
                        m = dve.scalar_tensor_tensor(delta[r, h, 0:DK], mo[r, h, 0:DK], rz[r, step - 1, h:h + 1],
                                                     v1[r, par, step - 1, h, 0:DK], ALU.mult, ALU.subtract, reverse1=True)
                    m.then_inc(delta_done[step - 1], 1)

            def memory_out(step, u, g):
                r, t = {1: (slice(0, SEG), 0), 2: (slice(0, SEG), 1), 3: (slice(SEG, P), 1)}[step]
                for h in range(2):
                    m = dve.scalar_tensor_tensor(attm[r, h, t], mo[r, h, 0:DK], rz[r, step - 1, h:h + 1],
                                                 beta[r, 2 * g + h], ALU.mult, ALU.mult)
                m.then_inc(attm_done[step - 1], 1)

            beta_of = None

            def slot(b, u, g, cur, nxt, prv):
                par = g % 2
                gp = (g - 1) % PAIRS
                if b is None:
                    dve.memset(v1[:, :, :, :, DK:VW], 1.0).then_inc(consts, 1)
                    dve.memset(delta[:, :, DK:VW], 1.0).then_inc(consts, 1)
                    dve.memset(z_start[:], 0.0).then_inc(ln_c, 1)
                    dve.wait_ge(ln_c, 1)
                    dve.memset(z_start[:, :, DK:VW], 1.0 / DK).then_inc(ln_c, 1)
                    dve.memset(attm[:], 0.0).then_inc(ln_c, 1)
                    dve.wait_ge(ln_c, 3)
                    dve.wait_ge(x_in_dma, 16)
                    dve.wait_ge(consts, 8)
                    norm_stats(ln1, x_in_t)
                    dve.wait_ge(ln1.stats_done, 2)
                    norm_guess(ln1, 0)
                    normalise(ln1, 0, x_in_t, xn_t, xn_done)
                    split_lo(0)
                    dve.wait_ge(beta_ready, 1)
                    dve.tensor_scalar(beta_rest[:], beta[:], -1.0, 1.0, ALU.mult, ALU.add).then_inc(beta_ready, 1)
                    turn_x_lo(0)
                    split_lo(1)
                if cur:
                    has(dve, sc, u)
                    dve.tensor_tensor(sm[:], TB[:, 0:4 * SEG].rearrange("p (j k) -> p j k", j=4),
                                      causal[:, None, :].broadcast_to([P, 4, SEG]), ALU.add).then_inc(masked, 1)
                    has(dve, masked, u)
                    dve.tensor_reduce(mx[:], sm[:], AX_X, ALU.max).then_inc(mx_done, 1)
                if prv:
                    use_memory(3, u - 1, 1 - par)
                    memory_out(3, u - 1, gp)
                if cur:
                    copy_memory(1, u)
                    use_memory(1, u, par)
                    has(dve, att_done, u - 1)
                    memory_out(1, u, g)
                    has(dve, pr_done, u)
                    for rows, cols in ((slice(0, SEG), slice(SEG, P)), (slice(SEG, P), slice(0, SEG))):
                        m = dve.tensor_reduce(rs[rows], pr[rows, :, cols], AX_X, ALU.add)
                    m.then_inc(sum_done, 1)
                    has(dve, sum_done, u)
                    dve.reciprocal(rr[:], rs[:]).then_inc(rr_done, 1)
                if cur:
                    copy_memory(2, u)
                if nxt:
                    sigma(0, u + 1, 1 - par)
                if cur:
                    use_memory(2, u, par)
                    memory_out(2, u, g)
                if nxt:
                    sigma(1, u + 1, 1 - par)
                half, routed = out_half(b, g), routed_half(b, g)
                more = cur and not (isinstance(b, int) and b == BATCH - 1)
                if more and g == PAIRS - 5:
                    has(dve, x_in_dma, b + 1, 16)
                    dve.wait_ge(causal_done, 1)
                    norm_stats(ln1, x_in_t)
                if routed is not None and g % 4 == 0:
                    norm_stats(ln2, [x2[:]])
                if more and g == PAIRS - 3:
                    normalise(ln1, b + 1, x_in_t, xn_t, xn_done)
                if more and g == PAIRS - 2:
                    turn_x_lo(b + 1)
                if routed is not None and g % 4 == 2:
                    normalise_x2(routed)
                if half is not None and g % 4 == 3:
                    residual(half)
                if routed is not None and g % 4 == 3:
                    keep_logits(routed)
                if cur:
                    if more and g == PAIRS - 5:
                        has(dve, ln1.stats_done, b + 1, 2)
                    if routed is not None and g % 4 == 0:
                        has(dve, ln2.stats_done, routed)
                    copy_memory(3, u)
                    if more and g == PAIRS - 5:
                        norm_guess(ln1, b + 1)
                    if routed is not None and g % 4 == 0:
                        norm_guess(ln2, routed)
                else:
                    for n in (TILES - 2, TILES - 1) if b is not None else ():
                        if n == TILES - 1:
                            residual(n)
                            has(dve, x2_done, n)
                            norm_stats(ln2, [x2[:]])
                        has(dve, ln2.stats_done, n)
                        norm_guess(ln2, n)
                        normalise_x2(n)
                        keep_logits(n)
                if b is not None and isinstance(u, int) and u + 2 < PAIRS:
                    split_lo(u + 2)

            run_slots(dve, slot)

        @block.gpsimd
        def _(pool):
            def rsqrt(ln, n):
                def step(ins, k):
                    ins.then_inc(ln.newton, 1)
                    pool.wait_ge(ln.newton, n * STEPS_POOL + k)

                has(pool, ln.guess, n, STEPS_DVE)
                for k in range(0, STEPS_POOL, 4):
                    step(pool.tensor_tensor(ln.t[:], ln.y[:], ln.y[:], ALU.mult), k + 1)
                    step(pool.tensor_tensor(ln.t[:], ln.t[:], ln.v[:], ALU.mult), k + 2)
                    step(pool.tensor_tensor(ln.t[:], ln.t[:], three_halves[:, 0:ln.tiles], ALU.add), k + 3)
                    step(pool.tensor_tensor(ln.y[:], ln.y[:], ln.t[:], ALU.mult), k + 4)

            def slot(b, u, g, cur, nxt, prv):
                if b is None:
                    pool.memset(ident[:], 0.0).then_inc(consts, 1)
                    pool.memset(causal[:], 0.0).then_inc(consts, 1)
                    pool.memset(pr[:], 0.0).then_inc(consts, 1)
                    pool.memset(three_halves[:], 1.5).then_inc(consts, 1)
                    pool.wait_ge(consts, 6)
                    pool.affine_select(out=ident[:], in_=ident[:], compare_op=ALU.not_equal, fill=1.0, base=0,
                                       pattern=[[-1, P]], channel_multiplier=1).then_inc(consts, 1)
                    pool.wait_ge(consts, 7)
                    pool.affine_select(out=causal[:], in_=causal[:], compare_op=ALU.is_ge, fill=MASKED, base=0,
                                       pattern=[[-1, SEG]], channel_multiplier=1).then_inc(causal_done, 1)
                    pool.wait_ge(causal_done, 1)
                    pool.affine_select(out=causal[SEG:P], in_=causal[SEG:P], compare_op=ALU.is_ge, fill=MASKED, base=0,
                                       pattern=[[-1, SEG]], channel_multiplier=1).then_inc(consts, 1)
                    pool.wait_ge(consts, 8)
                    rsqrt(ln1, 0)
                    pool.memset(empty[:], 0.0).then_inc(empty_done, 1)
                    pool.wait_ge(empty_done, 1)
                    pool.memset(empty[:, D:D + 1].bitcast(I32), NO_TOKEN).then_inc(empty_done, 1)
                    pool.wait_ge(beta_ready, 2)
                if cur:
                    has(pool, mx_done, u)
                    pool.tensor_tensor(sm[:], sm[:], mx[:, :, None].broadcast_to([P, 4, SEG]), ALU.subtract).then_inc(sub_done, 1)
                if prv:
                    has(pool, attm_done[2], u - 1)
                    has(pool, dotb_done, u - 1)
                    pool.tensor_tensor(att[:], att[:], attm[:], ALU.add).then_inc(att_done, 1)
                if cur and g == PAIRS - 4 and not (isinstance(b, int) and b == BATCH - 1):
                    rsqrt(ln1, b + 1)
                if routed_half(b, g) is not None and g % 4 == 1 and cur:
                    rsqrt(ln2, routed_half(b, g))
                if b is not None and not cur:
                    rsqrt(ln2, TILES - 2)
                    rsqrt(ln2, TILES - 1)
                if cur:
                    has(pool, dot_done, u)
                    pool.tensor_tensor(att[:], att[:], beta_rest[:, 2 * g:2 * g + 2, None, :].broadcast_to([P, 2, 2, DK]),
                                       ALU.mult).then_inc(dotb_done, 1)

            run_slots(pool, slot)


def experts(nc, logits, xn2_rows, gate_up, down, slot_rows, out):
    n_tiles = SLOTS // P
    RING = 4
    EARLY = EXPERTS - RING
    ctx = ExitStack()
    with ctx:
        def sb(name, shape, dt=F32):
            return ctx.enter_context(nc.sbuf_tensor(name, shape, dt))

        def bank(name):
            return ctx.enter_context(nc.psum_tensor(name, [P, 512], F32))

        def sem(name):
            return ctx.enter_context(nc.semaphore(name))

        gu_hi = sb("gu_hi", [P, EXPERTS, KC, 2 * INNER], F32R)
        gu_lo = sb("gu_lo", [P, EXPERTS, KC, 2 * INNER], F32R)
        dn = sb("dn", [P, EXPERTS, IC, D])
        ident2 = sb("ident2", [P, P])
        tile_expert = sb("tile_expert", [1, n_tiles], I32)
        gu_stage = [sb(f"gu_stage{i}", [P, KC, 2 * INNER]) for i in range(2)]
        w_dma = [sem("w_dma0"), sem("w_dma1")]
        gu_hi_done, gu_lo_done = sem("gu_hi_done"), sem("gu_lo_done")

        def load_weights(sp, e):
            if e >= 2:
                sp.wait_ge(gu_lo_done, e - 1)
            sp.dma_start(gu_stage[e % 2][:], gate_up[e]).then_inc(w_dma[e % 2], 16)
            sp.dma_start(dn[:, e], down[e]).then_inc(w_dma[e % 2], 16)

        def split_weights_hi(act, e):
            act.wait_ge(w_dma[e % 2], 32 * (e // 2 + 1))
            act.activation(gu_hi[:, e], gu_stage[e % 2][:], ACT.Copy).then_inc(gu_hi_done, 1)

        def split_weights_lo(dve, e):
            dve.wait_ge(gu_hi_done, e + 1)
            dve.tensor_tensor(gu_lo[:, e], gu_stage[e % 2][:], gu_hi[:, e], ALU.subtract).then_inc(gu_lo_done, 1)

        PX, PH = bank("PX"), bank("PH")
        PG, PU, PY = ([bank(f"{n}{i}") for i in range(2)] for n in ("PG", "PU", "PY"))

        with ExitStack() as early:
            def esb(name, shape, dt=F32):
                return early.enter_context(nc.sbuf_tensor(name, shape, dt))

            pay = esb("pay", [P, TILES, ROW])
            first_is = esb("first_is", [P, EXPERTS])
            before = esb("before", [P, P], BF16)
            all_ones = esb("all_ones", [P, P], BF16)
            m1, m2, r1, w1, w2 = (esb(n, [P, TILES]) for n in ("m1", "m2", "r1", "w1", "w2"))
            oh = [esb(f"oh{k}", [P, TILES, EXPERTS]) for k in range(2)]
            rest = esb("rest", [P, TILES, EXPERTS])
            chosen = esb("chosen", [P, TILES, EXPERTS], BF16)
            place = esb("place", [P, TILES, EXPERTS])
            count_i = esb("count_i", [P, EXPERTS], I32)
            tiles_f, ones8, ends, starts = (esb(n, [P, EXPERTS]) for n in ("tiles_f", "ones8", "ends", "starts"))
            pos = [esb(f"pos{k}", [P, TILES], I32) for k in range(2)]
            tile_no = esb("tile_no", [1, n_tiles, EXPERTS])
            tile_e = esb("tile_e", [1, n_tiles])

            made, pay_dma, rt, ex_done, ranks = (sem(n) for n in ("made", "pay_dma", "rt", "ex_done", "ranks"))
            scattered = [[sem("scattered0a"), sem("scattered0b")], [sem("scattered1")] * 2]
            diff_done = sem("diff_done")
            pos_done = sem("pos_done")

            with nc.Block() as block:
                @block.sync
                def _(sp):
                    sp.dma_start(pay[:, :, 0:D], xn2_rows.rearrange("n p d -> p n d")).then_inc(pay_dma, 16)
                    for e in range(EARLY + 2):
                        load_weights(sp, e)

                @block.tensor
                def _(pe):
                    pe.wait_ge(made, MADE)
                    pe.wait_ge(rt, 12)
                    flat = chosen[:].rearrange("p n e -> p (n e)")
                    w = TILES * EXPERTS
                    m = pe.matmul(PG[0][:, 0:w], before[:], flat, start=True, stop=True)
                    for d in range(1, TILES):
                        m = pe.matmul(PG[0][:, d * EXPERTS:w], all_ones[:], flat[:, 0:w - d * EXPERTS],
                                      start=False, stop=True, skip_group_check=True)
                    m.then_inc(ranks, 1)
                    for n in range(TILES):
                        m = pe.matmul(PG[1][:, 0:EXPERTS], all_ones[:], chosen[:, n], start=n == 0, stop=n == TILES - 1)
                    m.then_inc(ranks, 1)

                @block.scalar
                def _(act):
                    act.wait_ge(diff_done, 1)
                    act.activation(w2[:], m2[:], ACT.Exp).then_inc(ex_done, 1)
                    for e in range(EARLY):
                        split_weights_hi(act, e)

                @block.vector
                def _(dve):
                    k = [0]

                    def step(ins):
                        k[0] = k[0] + 1
                        ins.then_inc(rt, 1)
                        dve.wait_ge(rt, k[0])

                    def wide(a):
                        return a[:, :, None].broadcast_to([P, TILES, EXPERTS])

                    dve.wait_ge(made, MADE)
                    lowest = first_is[:, None, :].broadcast_to([P, TILES, EXPERTS])
                    step(dve.tensor_reduce(m1[:], logits[:], AX_X, ALU.max))
                    for i, (src, best) in enumerate(((logits, m1), (rest, m2))):
                        step(dve.tensor_tensor(oh[i][:], src[:], wide(best), ALU.is_equal))
                        step(dve.tensor_tensor(oh[i][:], oh[i][:], lowest, ALU.mult))
                        step(dve.tensor_reduce(r1[:], oh[i][:], AX_X, ALU.max))
                        step(dve.tensor_tensor(oh[i][:], oh[i][:], wide(r1), ALU.is_equal))
                        if i == 0:
                            step(dve.scalar_tensor_tensor(rest[:], oh[0][:], -3e38, logits[:], ALU.mult, ALU.add))
                            step(dve.tensor_reduce(m2[:], rest[:], AX_X, ALU.max))
                    step(dve.tensor_tensor(chosen[:], oh[0][:], oh[1][:], ALU.add))
                    dve.tensor_tensor(m2[:], m2[:], m1[:], ALU.subtract).then_inc(diff_done, 1)
                    dve.wait_ge(ranks, 2)
                    step(dve.tensor_scalar(count_i[:], PG[1][:, 0:EXPERTS], 1.0, float(P - 1), ALU.max, ALU.add))
                    step(dve.tensor_scalar(count_i[:], count_i[:], 7, None, ALU.logical_shift_right))
                    step(dve.tensor_copy(tiles_f[:], count_i[:]))
                    step(dve.tensor_tensor_scan(ends[:], ones8[:], tiles_f[:], 0.0, ALU.mult, ALU.add))
                    step(dve.tensor_tensor(starts[:], ends[:], tiles_f[:], ALU.subtract))
                    step(dve.tensor_scalar(starts[:], starts[:], float(P), None, ALU.mult))
                    step(dve.tensor_tensor(place[:], PG[0][:, 0:TILES * EXPERTS].rearrange("p (n e) -> p n e", e=EXPERTS),
                                           starts[:, None, :].broadcast_to([P, TILES, EXPERTS]), ALU.add))
                    for i in range(2):
                        step(dve.tensor_tensor(oh[i][:], oh[i][:], place[:], ALU.mult))
                        step(dve.tensor_reduce(r1[:], oh[i][:], AX_X, ALU.add))
                        step(dve.tensor_copy(pos[i][:], r1[:]))
                    dve.wait_ge(ex_done, 1)
                    step(dve.tensor_scalar(r1[:], w2[:], 1.0, None, ALU.add))
                    step(dve.reciprocal(w1[:], r1[:]))
                    step(dve.tensor_tensor(w2[:], w2[:], w1[:], ALU.mult))
                    dve.wait_ge(pay_dma, 16)
                    dve.tensor_copy(pay[:, :, D + 1], w1[:]).then_inc(pos_done, 1)
                    step(dve.tensor_tensor(tile_no[:], tile_no[:], ends[0:1, None, :].broadcast_to([1, n_tiles, EXPERTS]), ALU.is_ge))
                    step(dve.tensor_reduce(tile_e[:], tile_no[:], AX_X, ALU.add))
                    step(dve.tensor_scalar(tile_expert[:], tile_e[:], float(EXPERTS - 1), None, ALU.min))
                    for e in range(EARLY):
                        split_weights_lo(dve, e)
                        if e < 2:
                            n = slice(e * TILES // 2, (e + 1) * TILES // 2)
                            dve.wait_ge(scattered[0][e], 8 * TILES)
                            dve.tensor_copy(pay[:, n, D + 1], w2[:, n]).then_inc(pos_done, 1)

                @block.gpsimd
                def _(pool):
                    pool.iota(tile_no[:], [[1, n_tiles], [0, EXPERTS]], base=0, channel_multiplier=0,
                              allow_small_or_imprecise_dtypes=True).then_inc(made, 1)
                    pool.iota(first_is[:], [[-1, EXPERTS]], base=EXPERTS, channel_multiplier=0,
                              allow_small_or_imprecise_dtypes=True).then_inc(made, 1)
                    pool.memset(all_ones[:], 1.0).then_inc(made, 1)
                    pool.memset(before[:], 1.0).then_inc(made, 1)
                    pool.memset(ones8[:], 1.0).then_inc(made, 1)
                    pool.memset(ident2[:], 0.0).then_inc(made, 1)
                    pool.wait_ge(made, 6)
                    pool.affine_select(out=before[:], in_=before[:], compare_op=ALU.is_gt, fill=0.0, base=0,
                                       pattern=[[1, P]], channel_multiplier=-1).then_inc(made, 1)
                    pool.wait_ge(made, 7)
                    pool.affine_select(out=ident2[:], in_=ident2[:], compare_op=ALU.not_equal, fill=1.0, base=0,
                                       pattern=[[-1, P]], channel_multiplier=1).then_inc(made, 1)
                    pool.wait_ge(pay_dma, 16)
                    pool.wait_ge(made, 8)
                    pool.iota(pay[:, :, D].bitcast(I32), [[P, TILES]], base=0, channel_multiplier=1).then_inc(made, 1)
                    pool.wait_ge(made, 9)
                    for i in range(2):
                        for n in range(TILES):
                            if i == 0 and n == 0:
                                pool.wait_ge(pos_done, 1)
                            if i == 1 and n % (TILES // 2) == 0:
                                pool.wait_ge(pos_done, 2 + 2 * n // TILES)
                            pool.indirect_dma_start(slot_rows, bass.IndirectOffsetOnAxis(ap=pos[i][:, n:n + 1].bitcast(U32), axis=0),
                                                    pay[:, n, :], None).then_inc(scattered[i][2 * n // TILES], 16)
                    pool.wait_ge(scattered[1][0], 16 * TILES)

        slot = [sb(f"slot{i}", [P, ROW]) for i in range(RING)]
        xT_hi = [sb(f"exT_hi{i}", [P, KC, P], F32R) for i in range(2)]
        xT_lo = [sb(f"exT_lo{i}", [P, KC, P], F32R) for i in range(2)]
        act_g = [sb(f"act_g{i}", [P, INNER]) for i in range(2)]
        hid = [sb(f"hid{i}", [P, INNER]) for i in range(2)]
        hidT = [sb(f"hidT{i}", [P, IC, P]) for i in range(2)]
        y = [sb(f"y{i}", [P, D]) for i in range(2)]
        row_of = [sb(f"row_of{i}", [P, 1], I32) for i in range(2)]
        zero_i = sb("zero_i", [P, 1], I32)
        indexed, zeroed = sem("m_indexed"), sem("m_zeroed")
        slot_dma = [sem(f"slot_dma{i}") for i in range(RING)]
        xt, xhi, xlo, gated, upped, silu, hid_done, ht, hidT_done, yt, y_done, added = (sem(n) for n in (
            "m_xt", "m_xhi", "m_xlo", "m_gated", "m_upped", "m_silu", "m_hid", "m_ht", "m_hidT", "m_yt", "m_y", "m_added"))

        def steps(engine, body):
            for q in range(RING):
                body(q, q, 0)
            with engine.Fori(1, n_tiles // RING - 1) as jj:
                for q in range(RING):
                    body(RING * jj + q, q, jj)
            for q in range(RING):
                body(n_tiles - RING + q, q, n_tiles // RING - 1)

        def loaded(eng, q, jj):
            eng.wait_ge(slot_dma[q % RING], (jj + q // RING + 1) * 16)

        def ends_of(j, q):
            return q % 2, isinstance(j, int) and j == 0, isinstance(j, int) and j == n_tiles - 1

        def has(eng, s, j):
            if isinstance(j, int) and j < 0:
                return
            eng.wait_ge(s, j + 1)

        with nc.Block() as block:
            @block.sync
            def _(sp):
                def load(j, i):
                    sp.dma_start(slot[i][:], slot_rows[bass.ds(j, P), :]).then_inc(slot_dma[i], 16)

                for q in range(RING):
                    load(q * P, q)

                def body(j, q, jj):
                    if isinstance(j, int) and j + RING >= n_tiles:
                        return
                    if isinstance(j, int) and EARLY + 2 + j < EXPERTS:
                        load_weights(sp, EARLY + 2 + j)
                    row, done = (v if isinstance(j, int) else sp.snap(v) for v in ((j + RING) * P, j + 1))
                    sp.wait_ge(xt, done)
                    sp.wait_ge(y_done, done)
                    sp.wait_ge(indexed, done)
                    load(row, q)

                steps(sp, body)

            @block.tensor
            def _(pe):
                def turn_x(j, q, jj):
                    loaded(pe, q, jj)
                    has(pe, xlo, j - 1)
                    for c in range(KC):
                        m = pe.transpose(PX[:, c * P:(c + 1) * P], slot[q % RING][:, c * P:(c + 1) * P], ident2[:])
                    m.then_inc(xt, 1)

                def body(j, q, jj):
                    i, first, last = ends_of(j, q)
                    if first:
                        turn_x(0, 0, 0)
                    if not last:
                        turn_x(j + 1, q + 1, jj)
                    e = pe.value_load(tile_expert[0:1, bass.ds(j, 1)], min_val=0, max_val=EXPERTS - 1)
                    has(pe, xlo, j)
                    if not (isinstance(j, int) and j < RING):
                        pe.wait_ge(gu_lo_done, e + 1)
                    if not first:
                        has(pe, hid_done, j - 2)
                    for half, dst, done in ((0, PG[i], gated), (1, PU[i], upped)):
                        cols = slice(half * INNER, (half + 1) * INNER)
                        for c in range(KC):
                            hi, lo = (w[:, bass.ds(e, 1), c, cols] for w in (gu_hi, gu_lo))
                            pe.matmul(dst[:], xT_hi[i][:, c], lo, start=c == 0, stop=False)
                            pe.matmul(dst[:], xT_hi[i][:, c], hi, start=False, stop=False)
                            m = pe.matmul(dst[:], xT_lo[i][:, c], hi, start=False, stop=c == KC - 1)
                        m.then_inc(done, 1)
                    if not first:
                        finish(j - 1, 1 - i)
                    if last:
                        finish(j, i)

                def finish(j, i):
                    e = pe.value_load(tile_expert[0:1, bass.ds(j, 1)], min_val=0, max_val=EXPERTS - 1)
                    has(pe, hid_done, j)
                    has(pe, hidT_done, j - 1)
                    for c in range(IC):
                        m = pe.transpose(PH[:, c * P:(c + 1) * P], hid[i][:, c * P:(c + 1) * P], ident2[:])
                    m.then_inc(ht, 1)
                    has(pe, hidT_done, j)
                    if not (isinstance(j, int) and j < 2):
                        has(pe, y_done, j - 2)
                    for c in range(IC):
                        m = pe.matmul(PY[i][:, 0:D], hidT[i][:, c], dn[:, bass.ds(e, 1), c, :], start=c == 0, stop=c == IC - 1)
                    m.then_inc(yt, 1)

                steps(pe, body)

            @block.scalar
            def _(act):
                def body(j, q, jj):
                    i, first, last = ends_of(j, q)
                    if first:
                        split(0, 0)
                    if not last:
                        split(j + 1, 1 - i)
                    if not first:
                        turned(j - 1, 1 - i)
                    has(act, gated, j)
                    has(act, hid_done, j - 2)
                    act.activation(act_g[i][:], PG[i][:], ACT.Silu).then_inc(silu, 1)
                    if isinstance(j, int) and j < RING:
                        split_weights_hi(act, EARLY + j)
                    if last:
                        turned(j, i)

                def split(j, i):
                    has(act, xt, j)
                    act.activation(xT_hi[i][:], PX[:, 0:KC * P], ACT.Copy).then_inc(xhi, 1)

                def turned(j, i):
                    has(act, ht, j)
                    act.activation(hidT[i][:], PH[:], ACT.Copy).then_inc(hidT_done, 1)

                steps(act, body)

            @block.vector
            def _(dve):
                def body(j, q, jj):
                    i, first, last = ends_of(j, q)
                    if first:
                        split(0, 0)
                    if not last:
                        split(j + 1, 1 - i)
                    if not first:
                        weigh(j - 1, q - 1)
                    has(dve, silu, j)
                    has(dve, upped, j)
                    if not first:
                        has(dve, ht, j - 2)
                    dve.tensor_tensor(hid[i][:], act_g[i][:], PU[i][:], ALU.mult).then_inc(hid_done, 1)
                    if isinstance(j, int) and j < RING:
                        split_weights_lo(dve, EARLY + j)
                    if last:
                        weigh(j, q)

                def split(j, i):
                    has(dve, xhi, j)
                    dve.tensor_tensor(xT_lo[i][:], PX[:, 0:KC * P], xT_hi[i][:], ALU.subtract).then_inc(xlo, 1)

                def weigh(j, q):
                    i = q % 2
                    has(dve, yt, j)
                    if not (isinstance(j, int) and j < 2):
                        dve.wait_ge(added, (j - 1) * 16)
                    dve.tensor_scalar(y[i][:], PY[i][:, 0:D], slot[q % RING][:, D + 1:D + 2], None, ALU.mult).then_inc(y_done, 1)

                steps(dve, body)

            @block.gpsimd
            def _(pool):
                last_row = pool.to_reg(TILES * P - 1)
                pool.memset(zero_i[:], 0).then_inc(zeroed, 1)
                pool.wait_ge(zeroed, 1)

                def take_index(q, jj):
                    loaded(pool, q, jj)
                    pool.tensor_tensor(row_of[q % 2][:], slot[q % RING][:, D:D + 1].bitcast(I32), zero_i[:], ALU.add).then_inc(indexed, 1)

                def body(j, q, jj):
                    i, first, last = ends_of(j, q)
                    if first:
                        take_index(0, 0)
                    has(pool, indexed, j)
                    has(pool, y_done, j)
                    if not first:
                        pool.wait_ge(added, j * 16)
                    if not last:
                        take_index(q + 1, jj)
                    pool.indirect_dma_start(out, bass.IndirectOffsetOnAxis(ap=row_of[i][:].bitcast(U32), axis=0),
                                            y[i][:], None, bounds_check=last_row, oob_is_err=False,
                                            compute_op=ALU.add).then_inc(added, 16)

                steps(pool, body)
                pool.wait_ge(added, n_tiles * 16)


def program(nc, x_ln, x_res, Wqkv, Wo, betas, gate, gate_up, down, out):
    slot_rows = nc.dram_tensor("slot_rows", [SLOTS, ROW], F32, kind="Internal").ap()
    xn2_rows = nc.dram_tensor("xn2_rows", [TILES, P, D], F32, kind="Internal").ap()
    with nc.sbuf_tensor("logits", [P, TILES, EXPERTS], F32) as logits:
        attention(nc, x_ln, x_res, Wqkv, Wo, betas, gate, logits, out, xn2_rows, slot_rows)
        experts(nc, logits, xn2_rows, gate_up, down, slot_rows, out.rearrange("n p d -> (n p) d"))


SEGMENTS_IN = [0, 1, 3, 2]
SEGMENTS_OUT = [1, 0, 2, 3]


def kernel(**inputs):
    import concourse.bacc as bacc
    from concourse.bass_utils import run_bass_kernel_spmd

    a = {k: np.asarray(v) for k, v in inputs.items()}
    x = a["L0_attn_x"].reshape(BATCH, NSEG, SEG, D)
    by_pair = [a[f"L0_attn_W{c}"].reshape(KC, P, PAIRS, PW).transpose(2, 1, 0, 3) for c in "qkv"]
    half = HEADS // 2 * 4
    arrays = {
        "x_ln": x[:, SEGMENTS_IN].reshape(BATCH, 2, P, D).transpose(0, 2, 1, 3),
        "x_res": x.reshape(BATCH, NSEG, 2, half, D)[:, SEGMENTS_OUT].transpose(0, 2, 1, 3, 4).reshape(TILES, P, D),
        "Wqkv": np.stack(by_pair, 2),
        "Wo": a["L0_attn_Wo"].reshape(HEADS, DK, D).transpose(1, 0, 2),
        "betas": a["L0_attn_betas"].reshape(HEADS, DK),
        "gate": a["L0_ffn_gate_weight"].T.reshape(KC, P, EXPERTS).transpose(1, 0, 2),
        "gate_up": a["L0_ffn_gate_up_proj"].reshape(EXPERTS, 2 * INNER, KC, P).transpose(0, 3, 2, 1),
        "down": a["L0_ffn_down_proj"].reshape(EXPERTS, D, IC, P).transpose(0, 3, 2, 1),
    }
    arrays = {k: np.ascontiguousarray(v) for k, v in arrays.items()}
    nc = bacc.Bacc("TRN2", target_bir_lowering=False, num_devices=1)
    args = [nc.dram_tensor(k, v.shape, mybir.dt.from_np(v.dtype), kind="ExternalInput").ap() for k, v in arrays.items()]
    out = nc.dram_tensor("out", (TILES, P, D), F32, kind="ExternalOutput").ap()
    program(nc, *args, out)
    got = run_bass_kernel_spmd(nc, [arrays], core_ids=[0]).results[0]["out"]
    back = np.argsort(SEGMENTS_OUT)
    got = got.reshape(BATCH, 2, NSEG, half, D).transpose(0, 2, 1, 3, 4)[:, back]
    return np.ascontiguousarray(got.reshape(BATCH, SEQ, D))
```

```python
from contextlib import ExitStack

import numpy as np
import concourse.bass as bass
import concourse.mybir as mybir

F32 = mybir.dt.float32
F32R = mybir.dt.float32r
BF16 = mybir.dt.bfloat16
I32 = mybir.dt.int32
U32 = mybir.dt.uint32
ALU = mybir.AluOpType
ACT = mybir.ActivationFunctionType
AX_X = mybir.AxisListType.X

P = 128
BATCH, SEQ, D = 8, 256, 256
HEADS, DK, SEG = 16, 128, 64
NSEG = SEQ // SEG
PAIRS = HEADS // 2
UNITS = BATCH * PAIRS
TILES = BATCH * SEQ // P
KC = D // P
PW = 2 * P
VW = DK + 1
EPS = 1e-5
MASKED = -1e30
EXPERTS, INNER = 8, 512
IC = INNER // P
STEPS_DVE, STEPS_POOL = 5, 12
WG = 3 * KC * PW
WX = 2 * INNER * KC
ROW = D + 2
REGION = TILES * P + P
N_TILES = (2 * BATCH * SEQ + EXPERTS * (P - 1)) // P
SPARE = (N_TILES - 2 * TILES) * P
SLOTS = EXPERTS * REGION + SPARE
CHOOSE, ADDRESS = 9, 6
NO_TOKEN = 1 << 30
RSQRT_GUESS = float(0x5F3759DF)


class Slots:

    def __init__(self, nc, ctx):
        def sb(name, shape, dt=F32):
            return ctx.enter_context(nc.sbuf_tensor(name, shape, dt))

        self.rows = nc.dram_tensor("slot_rows", [SLOTS, ROW], F32, kind="Internal").ap()
        self.pay = sb("pay", [P, 2, ROW])
        self.pos = sb("pos", [P, 2], I32)
        self.filled = sb("filled", [P, EXPERTS])
        self.filled_i = sb("filled_i", [P, EXPERTS], I32)
        self.empty = sb("empty", [P, ROW])
        self.tile_expert = sb("tile_expert", [1, N_TILES], I32)
        self.tile_row = sb("tile_row", [1, N_TILES], I32)
        self.scattered = [ctx.enter_context(nc.semaphore(n)) for n in ("scattered_first", "scattered_second")]
        self.pad_dma = ctx.enter_context(nc.semaphore("pad_dma"))


class Norm:

    def __init__(self, sb, sem, name, tiles):
        self.stats = sb(f"{name}_stats", [P, tiles, 6])
        self.mv = sb(f"{name}_mv", [P, tiles, 2])
        self.v = sb(f"{name}_v", [P, tiles])
        self.y = sb(f"{name}_y", [P, tiles])
        self.t = sb(f"{name}_t", [P, tiles])
        self.stats_done = sem(f"{name}_stats_done")
        self.guess = sem(f"{name}_guess")
        self.newton = sem(f"{name}_newton")
        self.here = sem(f"{name}_here")
        self.tiles = tiles


def attention(nc, x_ln, x_res, Wqkv, Wo, betas, gate, gate_up, x2_out, slots, hi, lo, ident):
    ctx = ExitStack()
    with ctx:
        def sb(name, shape, dt=F32):
            return ctx.enter_context(nc.sbuf_tensor(name, shape, dt))

        def bank(name):
            return ctx.enter_context(nc.psum_tensor(name, [P, 512], F32))

        def sem(name):
            return ctx.enter_context(nc.semaphore(name))

        slot_rows, pay, pos, empty = slots.rows, slots.pay, slots.pos, slots.empty
        filled, filled_i = slots.filled, slots.filled_i
        scattered, pad_dma = slots.scattered, slots.pad_dma

        causal = sb("causal", [P, SEG])
        three_halves = sb("three_halves", [P, 2])
        z_start = sb("z_start", [P, 2, VW])
        w_hi, w_lo = (w[:].rearrange("p g (m c n) -> p g m c n", m=3, c=KC) for w in (hi, lo))
        w_stage = [sb(f"w_stage{i}", [P, WG]) for i in range(2)]
        wo = sb("wo", [P, PAIRS, 2, D])
        beta = sb("beta", [P, PAIRS, 2, DK])
        beta_rest = sb("beta_rest", [P, PAIRS, 2, DK])
        x_in = sb("x_in", [P, 2, D])
        xn = sb("xn", [P, 2, D])
        xT_hi = sb("xT_hi", [P, KC, SEQ], F32R)
        xT_lo = sb("xT_lo", [P, KC, SEQ], F32R)
        xr = sb("xr", [P, D])
        x2 = sb("x2", [P, D])
        xn2T = sb("xn2T", [P, KC, P])
        gate_sb = sb("gate_sb", [P, KC, EXPERTS])
        before = sb("before", [P, P], BF16)
        all_ones = sb("all_ones", [P, P], BF16)
        lowest = sb("lowest", [P, EXPERTS])
        logits = sb("logits", [P, EXPERTS])
        rest = sb("rest", [P, EXPERTS])
        best = sb("best", [P, 2])
        tie = sb("tie", [P, 2])
        chosen = sb("chosen", [P, 2, EXPERTS])
        both = sb("both", [P, EXPERTS], BF16)
        gap = sb("gap", [P, 1])
        odds = sb("odds", [P, 1])
        odds1 = sb("odds1", [P, 1])
        weight2 = sb("weight2", [P, 1])
        place = sb("place", [P, EXPERTS])
        place2 = sb("place2", [P, 2, EXPERTS])
        pos_f = sb("pos_f", [P, 2])
        qk = sb("qk", [P, 2, 512])
        ex = sb("ex", [P, 2, 448])
        sig = sb("sig", [P, 2, 2, 448])
        v1 = sb("v1", [P, 2, 2, 2, VW])
        sk = sb("sk", [P, 2, 2, DK])
        mem = sb("mem", [P, 2, VW])
        delta = sb("delta", [P, 2, VW])
        rz = sb("rz", [P, 3, 2])
        sm = sb("sm", [P, 4, SEG])
        betas_in = sm[0:HEADS, 0:2].rearrange("p a b -> p (a b)")
        beta_rows = nc.dram_tensor("beta_rows", [HEADS, DK], F32, kind="Internal").ap()
        mx = sb("mx", [P, 4])
        pr = sb("pr", [P, 4, P])
        prT = sb("prT", [P, 4, P])
        rs = sb("rs", [P, 4])
        rr = sb("rr", [P, 4])
        att = sb("att", [P, 2, 2, DK])
        attm = sb("attm", [P, 2, 2, DK])
        aT = sb("aT", [P, 2, HEADS, P])

        tile_no = sb("tile_no", [1, N_TILES, EXPERTS])
        tile_start = sb("tile_start", [1, N_TILES])
        ended = ex[0:1, 0, 0:N_TILES * EXPERTS].rearrange("p (n e) -> p n e", e=EXPERTS)
        tile_e, first_tile = (sb(n, [1, N_TILES]) for n in ("tile_e", "first_tile"))
        region_start, ones8, count, tiles_f, ends = (sb(n, [1, EXPERTS]) for n in ("region_start", "ones8", "count", "tiles_f", "ends"))
        count_i = sb("count_i", [1, EXPERTS], I32)

        QK = [bank("QK0"), bank("QK1")]
        TA, TB, TC, MEM, MO, OUT = (bank(n) for n in ("TA", "TB", "TC", "MEM", "MO", "OUT"))
        mem_ps = MEM[:, 0:2 * VW].rearrange("p (h n) -> p h n", h=2)
        mo = MO[:, 0:2 * VW].rearrange("p (h n) -> p h n", h=2)

        consts = sem("consts")
        const_dma = sem("const_dma")
        beta_ready = sem("beta_ready")
        stage_in = [sem("stage_in0"), sem("stage_in1")]
        wo_dma = sem("wo_dma")
        w_hi_done = sem("w_hi_done")
        w_lo_done = sem("w_lo_done")
        x_in_dma, xr_dma, x2_dma = sem("x_in_dma"), sem("xr_dma"), sem("x2_dma")
        ln1, ln2 = Norm(sb, sem, "ln1", 2), Norm(sb, sem, "ln2", 1)
        empty_done, spare_dma, gate_dma = (sem(n) for n in ("empty_done", "spare_dma", "gate_dma"))
        rt_made, chose, chosen_done, gap_done, odds_done, ranked, placed, placed_read = (sem(n) for n in (
            "rt_made", "chose", "chosen_done", "gap_done", "odds_done", "ranked", "placed", "placed_read"))
        addressed, tok_done, w2_in, filled_done, before_set = (sem(n) for n in (
            "addressed", "tok_done", "w2_in", "filled_done", "before_set"))
        xn2_done, xn2t, xn2T_done, lg, lg_done = (sem(n) for n in ("xn2_done", "xn2t", "xn2T_done", "lg", "lg_done"))
        xn_done, xt_done, xT_hi_done, xT_lo_done = (sem(n) for n in ("xn_done", "xt_done", "xT_hi_done", "xT_lo_done"))
        skt, sc, sm1, sm2, sm3, upd0, upd1, upd2, vp, pt, pv, attt, op = (sem(n) for n in (
            "skt", "sc", "sm1", "sm2", "sm3", "upd0", "upd1", "upd2", "vp", "pt", "pv", "attt", "op"))
        proj = [sem("projA"), sem("projB")]
        qkc = [sem("qkcA"), sem("qkcB")]
        exd = [sem("exA"), sem("exB")]
        mind = [sem("minA"), sem("minB")]
        sigd = [sem("sigA"), sem("sigB")]
        sk_done, v_done, prT_done, aT_done = (sem(n) for n in ("sk_done", "v_done", "prT_done", "aT_done"))
        masked, mx_done, sub_done, pr_done, sum_done, rr_done = (sem(n) for n in (
            "masked", "mx_done", "sub_done", "pr_done", "sum_done", "rr_done"))
        mem_done = [sem(f"mem_done{i}") for i in (1, 2, 3)]
        rz_done = [sem(f"rz_done{i}") for i in (1, 2, 3)]
        delta_done = [sem(f"delta_done{i}") for i in (1, 2)]
        table_made, table = sem("table_made"), sem("table")
        attm_done = [sem(f"attm_done{i}") for i in (1, 2, 3)]
        dot_done, dotb_done, att_done = sem("dot_done"), sem("dotb_done"), sem("att_done")
        x2_done = sem("x2_done")
        starts_set, causal_done = sem("starts_set"), sem("causal_done")

        def has(eng, s, unit, each=1):
            if isinstance(unit, int) and unit < 0:
                return
            eng.wait_ge(s, (unit + 1) * each)

        block = ctx.enter_context(nc.Block())

        def out_half(b, g):
            return None if b is None or (isinstance(b, int) and 2 * b + g // 4 < 1) else 2 * b + g // 4 - 1

        def routed_half(b, g):
            return None if b is None or (isinstance(b, int) and b < 1) else 2 * b + g // 4 - 2

        def sent_half(b, g):
            return None if b is None or (isinstance(b, int) and 2 * b + g // 4 < 3) else 2 * b + g // 4 - 3

        def run_slots(engine, slot):
            slot(None, -1, PAIRS - 1, False, True, False)
            for g in range(PAIRS):
                slot(0, g, g, True, True, g > 0)
            for g in range(PAIRS):
                slot(1, PAIRS + g, g, True, True, True)
            with engine.Fori(2, BATCH - 1) as b:
                for g in range(PAIRS):
                    slot(b, b * PAIRS + g, g, True, True, True)
            for g in range(PAIRS):
                slot(BATCH - 1, (BATCH - 1) * PAIRS + g, g, True, g < PAIRS - 1, True)
            slot(BATCH, UNITS, 0, False, False, True)

        def fill_up(engine, experts):
            engine.wait_ge(filled_done, 1)
            for e in experts:
                end = engine.value_load(filled_i[0:1, e:e + 1], min_val=e * REGION, max_val=(e + 1) * REGION - P)
                engine.dma_start(slot_rows[bass.ds(end, P), :], empty[:]).then_inc(pad_dma, 16)

        @block.sync
        def _(sp):
            def stage(k):
                has(sp, w_lo_done, k - 2)
                sp.dma_start(w_stage[k % 2][:], Wqkv[k] if k < PAIRS else gate_up[k - PAIRS, :, 0:WG]).then_inc(stage_in[k % 2], 16)

            def load_x_in(b):
                has(sp, xn_done, b - 1)
                sp.dma_start(x_in[:], x_ln[b]).then_inc(x_in_dma, 16)

            def slot(b, u, g, cur, nxt, prv):
                if b is None:
                    load_x_in(0)
                    stage(0)
                    sp.dma_start(betas_in, betas).then_inc(const_dma, 16)
                    stage(1)
                    sp.wait_ge(beta_ready, 1)
                    sp.dma_start(beta_rows, betas_in).then_inc(const_dma, 16)
                    sp.wait_ge(const_dma, 32)
                    sp.dma_start(beta[:].rearrange("p g h d -> p (g h) d"), beta_rows.partition_broadcast(P)).then_inc(const_dma, 16)
                    stage(2)
                    sp.dma_start(wo[:], Wo).then_inc(wo_dma, 16)
                    sp.dma_start(gate_sb[:], gate).then_inc(gate_dma, 16)
                    sp.wait_ge(empty_done, 2)
                    sp.dma_start(slot_rows[EXPERTS * REGION:SLOTS, :].rearrange("(n p) r -> p n r", p=P),
                                 empty[:, None, :].broadcast_to([P, SPARE // P, ROW])).then_inc(spare_dma, 16)
                if b is not None and isinstance(u, int) and u + 3 < PAIRS:
                    stage(u + 3)
                if g == 1 and cur and not (isinstance(b, int) and b == BATCH - 1):
                    load_x_in(b + 1)
                if cur and isinstance(b, int) and b == BATCH - 1:
                    if g == 0:
                        stage(PAIRS)
                    if g < PAIRS - 1:
                        stage(PAIRS + g + 1)
                half = out_half(b, g)
                if half is None:
                    return
                if g % 4 == 0:
                    has(sp, x2_done, half - 1)
                    sp.dma_start(xr[:], x_res[half]).then_inc(xr_dma, 16)
                if g % 4 == 3 or not cur:
                    has(sp, x2_done, half)
                    sp.dma_start(x2_out[half], x2[:]).then_inc(x2_dma, 16)

            run_slots(sp, slot)
            fill_up(sp, range(0, EXPERTS, 2))
            sp.wait_ge(x2_dma, 16 * TILES)
            sp.wait_ge(spare_dma, 16)

        @block.tensor
        def _(pe):
            def exact(out, a_hi, a_lo, b_hi, b_lo, first, last, **kw):
                pe.matmul(out, a_hi, b_lo, start=first, stop=False, **kw)
                pe.matmul(out, a_hi, b_hi, start=False, stop=False, **kw)
                return pe.matmul(out, a_lo, b_hi, start=False, stop=last, **kw)

            def transpose_x(b):
                has(pe, xn_done, b)
                has(pe, exd[1], b * PAIRS - 1)
                has(pe, qkc[1], b * PAIRS - 1)
                for t in range(2):
                    for c in range(KC):
                        m = pe.transpose(QK[1][:, (2 * c + t) * P:(2 * c + t + 1) * P], xn[:, t, c * P:(c + 1) * P], ident[:])
                m.then_inc(xt_done, 1)

            def turn_xn2(n, par, u):
                has(pe, xn2_done, n)
                has(pe, exd[1], u + 1)
                has(pe, qkc[1], u + 1)
                for c in range(KC):
                    m = pe.transpose(QK[1][:, c * P:(c + 1) * P], pay[:, par, c * P:(c + 1) * P], ident[:])
                m.then_inc(xn2t, 1)

            def rank(n):
                has(pe, chosen_done, n)
                pe.matmul(QK[1][:, 0:EXPERTS], before[:], both[:], start=True, stop=True)
                pe.matmul(QK[1][:, EXPERTS:2 * EXPERTS], all_ones[:], both[:], start=True, stop=True).then_inc(ranked, 1)

            def route(n):
                has(pe, xn2T_done, n)
                for c in range(KC):
                    m = pe.matmul(QK[1][:, 0:EXPERTS], xn2T[:, c], gate_sb[:, c], start=c == 0, stop=c == KC - 1)
                m.then_inc(lg, 1)

            def project(h, u, gn, b, routed=None, sent=None):
                if h == 0:
                    has(pe, w_lo_done, gn if isinstance(u, int) and u < PAIRS else PAIRS - 1)
                    has(pe, xT_lo_done, b)
                has(pe, exd[h], u - 1)
                has(pe, qkc[h], u - 1)
                if h == 1 and gn == 0:
                    has(pe, xT_lo_done, b)
                if h == 1 and routed is not None:
                    has(pe, lg_done, routed)
                if h == 1 and sent is not None:
                    has(pe, placed, sent)
                blocks = QK[h][:, :].rearrange("p (s m t) -> p m s t", m=2, t=SEG)
                for m in range(2):
                    for c in range(KC):
                        a = slice(h * P, (h + 1) * P)
                        mm = exact(blocks[:, m], w_hi[:, gn, m, c, a], w_lo[:, gn, m, c, a],
                                   xT_hi[:, c, :], xT_lo[:, c, :], c == 0, c == KC - 1)
                mm.then_inc(proj[h], 1)

            def project_v(u, gn):
                has(pe, sk_done, u - 1)
                for t in range(2):
                    for c in range(KC):
                        a = slice(t * P, (t + 1) * P)
                        mm = exact(TA[:, t * PW:(t + 1) * PW], xT_hi[:, c, a], xT_lo[:, c, a],
                                   w_hi[:, gn, 2, c, :], w_lo[:, gn, 2, c, :], c == 0, c == KC - 1)
                mm.then_inc(vp, 1)

            def sk_rows(u, par):
                has(pe, v_done, u)
                has(pe, sigd[1], u)
                for h in range(2):
                    s = sig[:, par, h]
                    pe.transpose(TA[:, (2 * h) * P:(2 * h + 1) * P], s[:, 64:192], ident[:])
                    pe.transpose(TA[0:SEG, (2 * h) * P:(2 * h + 1) * P], s[:, 0:64], ident[:])
                    m = pe.transpose(TA[:, (2 * h + 1) * P:(2 * h + 2) * P], s[:, 320:448], ident[:])
                m.then_inc(skt, 1)

            def scores(u):
                has(pe, prT_done, u - 1)
                for h in range(2):
                    for s, (blk, row, t) in enumerate(((0, 64, 0), (1, 0, 0), (3, 0, 1), (2, 64, 1))):
                        q = qk[:, h, blk * 128:blk * 128 + SEG]
                        k = qk[:, h, blk * 128 + SEG:blk * 128 + 2 * SEG]
                        o = (2 * h + t) * SEG
                        m = pe.matmul(TB[row:row + SEG, o:o + SEG], q, k, start=True, stop=True)
                m.then_inc(sc, 1)

            def update(step, u, par):
                if step == 0:
                    has(pe, sk_done, u)
                    has(pe, mem_done[2], u - 1)
                else:
                    has(pe, delta_done[step - 1], u)
                rows = slice(0, SEG) if step == 0 else slice(SEG, P)
                for h in range(2):
                    d = v1[rows, par, 0, h] if step == 0 else delta[rows, h]
                    m = pe.matmul(mem_ps[:, h], sk[rows, h, step // 2], d, start=(step == 0 and h == 0),
                                  stop=(step == 2), skip_group_check=True)
                m.then_inc((upd0, upd1, upd2)[step], 1)

            def read_memory(step, u, par):
                has(pe, mem_done[step - 1], u)
                if step == 1:
                    has(pe, attm_done[2], u - 1)
                else:
                    has(pe, attm_done[step - 2], u)
                for h in range(2):
                    s = sig[:, par, h]
                    if step == 3:
                        m = pe.matmul(mo[SEG:P, h], s[:, 192:256], mem[:, h], start=True, stop=True)
                    else:
                        o = 64 if step == 1 else 320
                        m = pe.matmul(mo[:, h], s[:, o:o + P], mem[:, h], start=True, stop=True)
                m.then_inc((sm1, sm2, sm3)[step - 1], 1)

            def turn_att(u):
                has(pe, att_done, u)
                for h in range(2):
                    for t in range(2):
                        o = (2 * h + t) * P
                        m = pe.transpose(TC[:, o:o + P], att[:, h, t], ident[:])
                m.then_inc(attt, 1)

            def turn_probs(u):
                has(pe, pr_done, u)
                for j in range(4):
                    m = pe.transpose(TB[:, j * P:(j + 1) * P], pr[:, j], ident[:])
                m.then_inc(pt, 1)

            def probs_v(u, par):
                has(pe, prT_done, u)
                has(pe, aT_done, u - 1)
                for h in range(2):
                    for t in range(2):
                        o = (2 * h + t) * P
                        m = pe.matmul(TC[:, o:o + P], prT[:, 2 * h + t], v1[:, par, t, h, 0:DK], start=True, stop=True)
                m.then_inc(pv, 1)

            def project_out(part, u, half, g, steps):
                if isinstance(half, int) and half == 0 and g == 4:
                    pe.wait_ge(wo_dma, 16)
                if part == 0 and g % 4 == 0:
                    has(pe, aT_done, u)
                    has(pe, x2_done, half - 1)
                for m in steps:
                    mm = pe.matmul(OUT[:, 0:D], aT[:, (g // 4 + 1) % 2, m], wo[:, m // 2, m % 2], start=m == 0, stop=m == HEADS - 1)
                    if m == HEADS - 1:
                        mm.then_inc(op, 1)

            def finish(half):
                quarters = [range(k, k + HEADS // 4) for k in range(0, HEADS, HEADS // 4)]
                project_out(0, UNITS - 1, half, 0, quarters[0])
                rank(TILES - 3)
                project_out(1, UNITS - 1, half, 0, quarters[1])
                has(pe, placed, TILES - 3)
                turn_xn2(TILES - 2, TILES % 2, UNITS - 2)
                project_out(2, UNITS - 1, half, 0, quarters[2][:2])
                route(TILES - 2)
                project_out(2, UNITS - 1, half, 0, quarters[2][2:])
                project_out(3, UNITS - 1, half, 0, quarters[3])
                rank(TILES - 2)
                has(pe, placed, TILES - 2)
                turn_xn2(TILES - 1, (TILES - 1) % 2, UNITS - 2)
                route(TILES - 1)
                rank(TILES - 1)

            def slot(b, u, g, cur, nxt, prv):
                par, gn = g % 2, (g + 1) % PAIRS
                if b is None:
                    pe.wait_ge(consts, 8)
                    transpose_x(0)
                bn = 0 if b is None else (b + 1 if g == PAIRS - 1 else b)
                half = out_half(b, g)
                steps = range(g % 4 * 4, g % 4 * 4 + 4) if cur else range(HEADS)
                if cur:
                    sk_rows(u, par)
                    scores(u)
                if prv:
                    read_memory(3, u - 1, 1 - par)
                if nxt:
                    project(0, u + 1, gn, bn)
                if cur:
                    update(0, u, par)
                if nxt:
                    project(1, u + 1, gn, bn, sent_half(b, g) if g % 4 == 0 else None,
                            sent_half(b, g) if g % 4 == 2 else None)
                if cur:
                    read_memory(1, u, par)
                if prv:
                    turn_att(u - 1)
                if nxt:
                    project_v(u + 1, gn)
                if cur:
                    update(1, u, par)
                    turn_probs(u)
                routed = routed_half(b, g)
                if isinstance(b, int) and b == 1 and g == 3:
                    pe.wait_ge(gate_dma, 16)
                    pe.wait_ge(rt_made, 5)
                if cur and routed is not None and g % 4 == 3:
                    turn_xn2(routed, g // 4, u if nxt else u - 1)
                if half is not None and cur:
                    project_out(0, u - 1, half, g, steps[:len(steps) // 2])
                if b is not None and not cur:
                    finish(half)
                if cur:
                    read_memory(2, u, par)
                    probs_v(u, par)
                if g == PAIRS - 2 and cur and not (isinstance(b, int) and b == BATCH - 1):
                    transpose_x(b + 1)
                if half is not None and cur:
                    project_out(1, u - 1, half, g, steps[len(steps) // 2:])
                if cur and routed is not None and g % 4 == 3:
                    route(routed)
                if cur and sent_half(b, g) is not None and g % 4 == 1:
                    has(pe, exd[1], u + 1)
                    has(pe, qkc[1], u + 1)
                    rank(sent_half(b, g))
                if cur:
                    update(2, u, par)

            run_slots(pe, slot)

        @block.scalar
        def _(act):
            def split_hi(k):
                act.wait_ge(stage_in[k % 2], 16 * (k // 2 + 1))
                act.activation(hi[:, k % PAIRS], w_stage[k % 2][:], ACT.Copy).then_inc(w_hi_done, 1)

            def weigh(n):
                has(act, gap_done, n)
                act.activation(odds[:], gap[:], ACT.Exp).then_inc(odds_done, 1)

            def slot(b, u, g, cur, nxt, prv):
                par = g % 2
                if b is None:
                    act.wait_ge(const_dma, 16)
                    act.activation(betas_in, betas_in, ACT.Sigmoid).then_inc(beta_ready, 1)
                    split_hi(0)
                    turn_x_hi(0)
                    split_hi(1)
                if cur:
                    has(act, skt, u)
                    act.activation(sk[:], TA[:, :], ACT.Copy).then_inc(sk_done, 1)
                for h in range(2):
                    if nxt:
                        has(act, proj[h], u + 1)
                        act.activation(qk[:, h], QK[h][:, :], ACT.Copy).then_inc(qkc[h], 1)
                        act.activation(ex[:, h], QK[h][:, 64:512], ACT.Exp).then_inc(exd[h], 1)
                    if h == 0 and cur:
                        has(act, sub_done, u)
                        for rows, cols in ((slice(0, SEG), slice(SEG, P)), (slice(SEG, P), slice(0, SEG))):
                            m = act.activation(pr[rows, :, cols], sm[rows], ACT.Exp, scale=float(DK) ** -0.5)
                        m.then_inc(pr_done, 1)
                if prv:
                    has(act, attt, u - 1)
                    gp = (g - 1) % PAIRS
                    for h in range(2):
                        row = (2 * gp + h) % PAIRS * 4
                        m = act.activation(aT[:, gp // 4, :, :].rearrange("p m (s r) -> p s r m", s=NSEG)[:, :, row:row + 4],
                                           TC[:, h * SEQ:(h + 1) * SEQ].rearrange("p (s i m) -> p s i m", s=NSEG, i=4), ACT.Copy)
                    m.then_inc(aT_done, 1)
                if nxt:
                    has(act, vp, u + 1)
                    act.activation(v1[:, 1 - par, :, :, 0:DK], TA[:, :].rearrange("p (t h n) -> p t h n", t=2, h=2),
                                   ACT.Copy).then_inc(v_done, 1)
                if cur:
                    has(act, pt, u)
                    act.activation(prT[:], TB[:, :], ACT.Copy).then_inc(prT_done, 1)
                    if routed_half(b, g) is not None and g % 4 == 3:
                        keep_xn2T(routed_half(b, g))
                    has(act, pv, u)
                    has(act, rr_done, u)
                    for h in range(2):
                        for t in range(2):
                            j = 2 * h + t
                            m = act.activation(att[:, h, t], TC[:, j * P:(j + 1) * P], ACT.Copy, scale=rr[:, j:j + 1])
                    m.then_inc(dot_done, 1)
                if g == PAIRS - 2 and cur and not (isinstance(b, int) and b == BATCH - 1):
                    turn_x_hi(b + 1)
                if sent_half(b, g) is not None and g % 4 == 1 and cur:
                    weigh(sent_half(b, g))
                if b is not None and not cur:
                    weigh(TILES - 3)
                    for n in (TILES - 2, TILES - 1):
                        keep_xn2T(n)
                        weigh(n)
                if cur and isinstance(b, int) and b == BATCH - 1:
                    split_hi(PAIRS + g)
                if isinstance(u, int) and u + 3 < PAIRS:
                    split_hi(u + 3)

            def keep_xn2T(n):
                has(act, xn2t, n)
                act.activation(xn2T[:], QK[1][:, 0:KC * P], ACT.Copy).then_inc(xn2T_done, 1)

            def turn_x_hi(b):
                has(act, xt_done, b)
                act.activation(xT_hi[:], QK[1][:, :], ACT.Copy).then_inc(xT_hi_done, 1)

            run_slots(act, slot)
            fill_up(act, range(1, EXPERTS, 2))

        @block.vector
        def _(dve):
            def split_lo(k, part=None):
                cols = slice(0, WG) if part is None else slice(part * WG // 2, (part + 1) * WG // 2)
                has(dve, w_hi_done, k)
                m = dve.tensor_tensor(lo[:, k % PAIRS, cols], w_stage[k % 2][:, cols], hi[:, k % PAIRS, cols], ALU.subtract)
                if part != 0:
                    m.then_inc(w_lo_done, 1)

            def split_in(b, u, g):
                if isinstance(b, int) and b == 0 and g + 2 < PAIRS:
                    return g + 2
                if isinstance(b, int) and b == BATCH - 1 and 0 < g < PAIRS - 1:
                    return PAIRS + g - 1
                return None

            def norm_stats(ln, src):
                for t in range(ln.tiles):
                    dve.bn_stats(ln.stats[:, t], src[t]).then_inc(ln.stats_done, 1)

            def norm_guess(ln, n):
                def step(ins, k):
                    ins.then_inc(ln.guess, 1)
                    dve.wait_ge(ln.guess, n * STEPS_DVE + k)

                for t in range(ln.tiles):
                    m = dve.bn_aggr(ln.mv[:, t], ln.stats[:, t])
                step(m, 1)
                step(dve.tensor_scalar(ln.v[:], ln.mv[:, :, 1], EPS, None, ALU.add), 2)
                step(dve.tensor_scalar(ln.y[:].bitcast(I32), ln.v[:].bitcast(I32), 1, None, ALU.logical_shift_right), 3)
                dve.tensor_scalar(ln.y[:].bitcast(I32), ln.y[:].bitcast(I32), -1.0, RSQRT_GUESS, ALU.mult, ALU.add).then_inc(ln.guess, 1)
                dve.tensor_scalar(ln.v[:], ln.v[:], -0.5, None, ALU.mult).then_inc(ln.guess, 1)

            def rsqrt_now(ln, n):
                dve.wait_ge(ln.guess, (n + 1) * STEPS_DVE)
                for k in range(3):
                    for t in range(ln.tiles):
                        y, v, w = (a[:, t:t + 1] for a in (ln.y, ln.v, ln.t))
                        m = dve.scalar_tensor_tensor(w, y, v, y, ALU.mult, ALU.mult)
                    m.then_inc(ln.here, 1)
                    dve.wait_ge(ln.here, 2 * k + 1)
                    m = dve.scalar_tensor_tensor(ln.y[:], ln.t[:], 1.5, ln.y[:], ALU.add, ALU.mult)
                    if k < 2:
                        m.then_inc(ln.here, 1)
                        dve.wait_ge(ln.here, 2 * k + 2)
                m.then_inc(ln.newton, STEPS_POOL)

            def normalise(ln, n, src, dst, done):
                has(dve, ln.newton, n, STEPS_POOL)
                for t in range(ln.tiles):
                    m = dve.tensor_scalar(dst[t], src[t], ln.mv[:, t, 0:1], ln.y[:, t:t + 1], ALU.subtract, ALU.mult)
                m.then_inc(done, 1)

            x_in_t, xn_t = [x_in[:, t] for t in range(2)], [xn[:, t] for t in range(2)]

            def normalise_x2(n, par):
                if not (isinstance(n, int) and n < 2):
                    dve.wait_ge(scattered[1], (n - 1) * 16)
                normalise(ln2, n, [x2[:]], [pay[:, par, 0:D]], xn2_done)
                token = pay[:, par, D:D + 1].bitcast(I32)
                dve.tensor_scalar(token, token, float(2 * P), None, ALU.add).then_inc(tok_done, 1)

            def keep_logits(n):
                has(dve, lg, n)
                dve.tensor_scalar(logits[:], QK[1][:, 0:EXPERTS], 1.0, None, ALU.mult).then_inc(lg_done, 1)

            def choose(n, part):
                def step(ins, k):
                    ins.then_inc(chose, 1)
                    dve.wait_ge(chose, n * CHOOSE + k)

                one = chosen[:, part]
                if part == 0:
                    has(dve, lg_done, n)
                    step(dve.tensor_reduce(best[:, 0:1], logits[:], AX_X, ALU.max), 1)
                else:
                    dve.wait_ge(chose, n * CHOOSE + 6)
                src, k = (logits, rest)[part], 1 + 5 * part
                step(dve.scalar_tensor_tensor(one, src[:], best[:, part:part + 1], lowest[:], ALU.is_equal, ALU.mult), k + 1)
                step(dve.tensor_reduce(tie[:, part:part + 1], one, AX_X, ALU.max), k + 2)
                step(dve.tensor_scalar(one, one, tie[:, part:part + 1], None, ALU.is_equal), k + 3)
                if part == 0:
                    step(dve.scalar_tensor_tensor(rest[:], one, -3e38, logits[:], ALU.mult, ALU.add), 5)
                    dve.tensor_reduce(best[:, 1:2], rest[:], AX_X, ALU.max).then_inc(chose, 1)
                else:
                    has(dve, ranked, n - 1)
                    dve.tensor_tensor(both[:], chosen[:, 0], chosen[:, 1], ALU.add).then_inc(chosen_done, 1)
                    dve.tensor_tensor(gap[:], best[:, 1:2], best[:, 0:1], ALU.subtract).then_inc(gap_done, 1)

            def find_places(n):
                has(dve, ranked, n)
                has(dve, placed, n - 1)
                dve.tensor_tensor(place[:], QK[1][:, 0:EXPERTS], filled[:], ALU.add).then_inc(placed_read, 1)
                dve.tensor_tensor(filled[:], QK[1][:, EXPERTS:2 * EXPERTS], filled[:], ALU.add).then_inc(placed, 1)

            def step_address(ins, n, k):
                ins.then_inc(addressed, 1)
                dve.wait_ge(addressed, n * ADDRESS + k)

            def weigh_choices(n, par):
                has(dve, odds_done, n)
                has(dve, scattered[1], n - 1, 16)
                step_address(dve.tensor_scalar(odds1[:], odds[:], 1.0, None, ALU.add), n, 1)
                step_address(dve.reciprocal(pay[:, par, D + 1:D + 2], odds1[:]), n, 2)
                w2 = pay[:, 1 - par, D + 1:D + 2] if isinstance(n, int) and n == TILES - 1 else weight2[:]
                step_address(dve.tensor_tensor(w2, odds[:], pay[:, par, D + 1:D + 2], ALU.mult), n, 3)

            def address(n):
                has(dve, placed_read, n)
                has(dve, tok_done, n)
                step_address(dve.tensor_tensor(place2[:], chosen[:], place[:, None, :].broadcast_to([P, 2, EXPERTS]), ALU.mult), n, 4)
                step_address(dve.tensor_reduce(pos_f[:], place2[:], AX_X, ALU.add), n, 5)
                dve.tensor_copy(pos[:], pos_f[:]).then_inc(addressed, 1)

            def second_weight(n, par):
                has(dve, scattered[0], n, 16)
                dve.tensor_scalar(pay[:, par, D + 1:D + 2], weight2[:], 1.0, None, ALU.mult).then_inc(w2_in, 1)

            def send(n, par):
                choose(n, 0)
                choose(n, 1)
                weigh_choices(n, par)
                if n == TILES - 1:
                    token, other = (pay[:, q, D:D + 1].bitcast(I32) for q in (par, 1 - par))
                    has(dve, tok_done, n)
                    has(dve, xn2_done, n)
                    dve.tensor_scalar(other, token, 0.0, None, ALU.add).then_inc(tok_done, 1)
                    dve.tensor_scalar(pay[:, 1 - par, 0:D], pay[:, par, 0:D], 1.0, None, ALU.mult).then_inc(tok_done, 1)
                find_places(n)
                if n == TILES - 1:
                    has(dve, placed, n)
                    dve.tensor_copy(filled_i[:], filled[:]).then_inc(filled_done, 1)
                    dve.wait_ge(tok_done, n + 3)
                address(n)

            def make_table():
                k = [0]

                def step(ins):
                    k[0] = k[0] + 1
                    ins.then_inc(table, 1)
                    dve.wait_ge(table, k[0])

                has(dve, placed, TILES - 1)
                dve.wait_ge(table_made, 4)
                step(dve.tensor_tensor(count[:], filled[0:1, :], region_start[:], ALU.subtract))
                step(dve.tensor_scalar(count_i[:], count[:], 1.0, float(P - 1), ALU.max, ALU.add))
                step(dve.tensor_scalar(count_i[:], count_i[:], 7, None, ALU.logical_shift_right))
                step(dve.tensor_copy(tiles_f[:], count_i[:]))
                step(dve.tensor_tensor_scan(ends[:], ones8[:], tiles_f[:], 0.0, ALU.mult, ALU.add))
                each = ends[:, None, :].broadcast_to([1, N_TILES, EXPERTS])
                step(dve.tensor_tensor(ended, tile_no[:], each, ALU.is_ge))
                step(dve.tensor_tensor(tile_no[:], ended, each, ALU.mult))
                step(dve.tensor_reduce(tile_e[:], ended, AX_X, ALU.add))
                step(dve.tensor_reduce(first_tile[:], tile_no[:], AX_X, ALU.max))
                step(dve.scalar_tensor_tensor(first_tile[:], first_tile[:], float(-P), tile_start[:], ALU.mult, ALU.add))
                dve.scalar_tensor_tensor(slots.tile_row[:], tile_e[:], float(REGION), first_tile[:], ALU.mult, ALU.add).then_inc(table, 1)
                dve.tensor_scalar(slots.tile_expert[:], tile_e[:], float(EXPERTS - 1), None, ALU.min).then_inc(table, 1)
                dve.wait_ge(table, k[0] + 2)

            def finish():
                last = TILES - 1
                norm_stats(ln2, [x2[:]])
                has(dve, ln2.stats_done, last - 1)
                norm_guess(ln2, last - 1)
                send(last - 2, last % 2)
                normalise_x2(last - 1, 1 - last % 2)
                second_weight(last - 2, last % 2)
                keep_logits(last - 1)
                send(last - 1, 1 - last % 2)
                residual(last)
                has(dve, x2_done, last)
                norm_stats(ln2, [x2[:]])
                has(dve, ln2.stats_done, last)
                norm_guess(ln2, last)
                rsqrt_now(ln2, last)
                normalise_x2(last, last % 2)
                split_lo(2 * PAIRS - 1)
                second_weight(last - 1, 1 - last % 2)
                keep_logits(last)
                send(last, last % 2)
                make_table()

            def residual(half):
                has(dve, op, half)
                has(dve, xr_dma, half, 16)
                has(dve, x2_dma, half - 1, 16)
                has(dve, xn2_done, half - 1)
                dve.tensor_tensor(x2[:], OUT[:, 0:D], xr[:], ALU.add).then_inc(x2_done, 1)

            def turn_x_lo(b):
                has(dve, xT_hi_done, b)
                dve.tensor_tensor(xT_lo[:], QK[1][:, :], xT_hi[:], ALU.subtract).then_inc(xT_lo_done, 1)

            def sigma(h, u, par):
                has(dve, exd[h], u)
                dve.tensor_scalar(ex[:, h], ex[:, h], 1.0, None, ALU.min).then_inc(mind[h], 1)
                has(dve, mind[h], u)
                dve.scalar_tensor_tensor(sig[:, par, h], qk[:, h, 64:512], 0.0, ex[:, h], ALU.max, ALU.add).then_inc(sigd[h], 1)

            def copy_memory(step, u):
                has(dve, (upd0, upd1, upd2)[step - 1], u)
                dve.tensor_tensor(mem[:], mem_ps, z_start[:], ALU.add).then_inc(mem_done[step - 1], 1)

            def use_memory(step, u, par):
                rows = {1: slice(0, P), 2: slice(0, P), 3: slice(SEG, P)}[step]
                has(dve, (sm1, sm2, sm3)[step - 1], u)
                dve.reciprocal(rz[rows, step - 1], mo[rows, :, DK]).then_inc(rz_done[step - 1], 1)
                has(dve, rz_done[step - 1], u)
                if step < 3:
                    for h in range(2):
                        r = slice(SEG, P)
                        m = dve.scalar_tensor_tensor(delta[r, h, 0:DK], mo[r, h, 0:DK], rz[r, step - 1, h:h + 1],
                                                     v1[r, par, step - 1, h, 0:DK], ALU.mult, ALU.subtract, reverse1=True)
                    m.then_inc(delta_done[step - 1], 1)

            def memory_out(step, u, g):
                r, t = {1: (slice(0, SEG), 0), 2: (slice(0, SEG), 1), 3: (slice(SEG, P), 1)}[step]
                for h in range(2):
                    m = dve.scalar_tensor_tensor(attm[r, h, t], mo[r, h, 0:DK], rz[r, step - 1, h:h + 1],
                                                 beta[r, g, h], ALU.mult, ALU.mult)
                m.then_inc(attm_done[step - 1], 1)

            def slot(b, u, g, cur, nxt, prv):
                par = g % 2
                gp = (g - 1) % PAIRS
                if b is None:
                    dve.memset(v1[:, :, :, :, DK:VW], 1.0).then_inc(consts, 1)
                    dve.memset(delta[:, :, DK:VW], 1.0).then_inc(consts, 1)
                    dve.memset(z_start[:], 0.0).then_inc(starts_set, 1)
                    dve.wait_ge(starts_set, 1)
                    dve.memset(z_start[:, :, DK:VW], 1.0 / DK).then_inc(starts_set, 1)
                    dve.memset(attm[:], 0.0).then_inc(starts_set, 1)
                    dve.wait_ge(starts_set, 3)
                    dve.wait_ge(x_in_dma, 16)
                    dve.wait_ge(consts, 8)
                    norm_stats(ln1, x_in_t)
                    dve.wait_ge(ln1.stats_done, 2)
                    norm_guess(ln1, 0)
                    rsqrt_now(ln1, 0)
                    normalise(ln1, 0, x_in_t, xn_t, xn_done)
                    split_lo(0)
                    turn_x_lo(0)
                    split_lo(1)
                if isinstance(u, int) and u == 0:
                    dve.wait_ge(const_dma, 48)
                    dve.tensor_scalar(beta_rest[:], beta[:], -1.0, 1.0, ALU.mult, ALU.add).then_inc(beta_ready, 1)
                if cur and split_in(b, u, g) is not None:
                    split_lo(split_in(b, u, g), 0)
                if cur:
                    has(dve, sc, u)
                    dve.tensor_tensor(sm[:], TB[:, 0:4 * SEG].rearrange("p (j k) -> p j k", j=4),
                                      causal[:, None, :].broadcast_to([P, 4, SEG]), ALU.add).then_inc(masked, 1)
                    has(dve, masked, u)
                    dve.tensor_reduce(mx[:], sm[:], AX_X, ALU.max).then_inc(mx_done, 1)
                if prv:
                    use_memory(3, u - 1, 1 - par)
                    memory_out(3, u - 1, gp)
                if cur:
                    copy_memory(1, u)
                    if split_in(b, u, g) is not None:
                        split_lo(split_in(b, u, g), 1)
                    sent = sent_half(b, g)
                    if sent is not None:
                        if g % 4 < 2:
                            choose(sent, g % 4)
                        elif g % 4 == 2:
                            weigh_choices(sent, (g // 4 + 1) % 2)
                            address(sent)
                        else:
                            second_weight(sent, (g // 4 + 1) % 2)
                    use_memory(1, u, par)
                    has(dve, att_done, u - 1)
                    memory_out(1, u, g)
                    has(dve, pr_done, u)
                    for rows, cols in ((slice(0, SEG), slice(SEG, P)), (slice(SEG, P), slice(0, SEG))):
                        m = dve.tensor_reduce(rs[rows], pr[rows, :, cols], AX_X, ALU.add)
                    m.then_inc(sum_done, 1)
                    has(dve, sum_done, u)
                    dve.reciprocal(rr[:], rs[:]).then_inc(rr_done, 1)
                if cur:
                    copy_memory(2, u)
                if cur and isinstance(b, int) and b == BATCH - 1 and g == PAIRS - 1:
                    split_lo(2 * PAIRS - 2)
                if nxt:
                    sigma(0, u + 1, 1 - par)
                if cur:
                    use_memory(2, u, par)
                if nxt:
                    sigma(1, u + 1, 1 - par)
                if cur:
                    memory_out(2, u, g)
                half, routed = out_half(b, g), routed_half(b, g)
                more = cur and not (isinstance(b, int) and b == BATCH - 1)
                if more and g == PAIRS - 5:
                    has(dve, x_in_dma, b + 1, 16)
                    dve.wait_ge(causal_done, 1)
                    norm_stats(ln1, x_in_t)
                if routed is not None and g % 4 == 0 and cur:
                    norm_stats(ln2, [x2[:]])
                if more and g == PAIRS - 3:
                    normalise(ln1, b + 1, x_in_t, xn_t, xn_done)
                if more and g == PAIRS - 2:
                    turn_x_lo(b + 1)
                if routed is not None and g % 4 == 2:
                    normalise_x2(routed, g // 4)
                if cur:
                    if more and g == PAIRS - 5:
                        has(dve, ln1.stats_done, b + 1, 2)
                    if routed is not None and g % 4 == 0:
                        has(dve, ln2.stats_done, routed)
                    copy_memory(3, u)
                    if more and g == PAIRS - 5:
                        norm_guess(ln1, b + 1)
                    if routed is not None and g % 4 == 0:
                        norm_guess(ln2, routed)
                    if sent_half(b, g) is not None and g % 4 == 1:
                        find_places(sent_half(b, g))
                    if routed is not None and g % 4 == 3:
                        keep_logits(routed)
                    if half is not None and g % 4 == 3:
                        residual(half)
                elif b is not None:
                    finish()

            run_slots(dve, slot)

        @block.gpsimd
        def _(pool):
            def rsqrt(ln, n):
                def step(ins, k):
                    ins.then_inc(ln.newton, 1)
                    pool.wait_ge(ln.newton, n * STEPS_POOL + k)

                has(pool, ln.guess, n, STEPS_DVE)
                for k in range(0, STEPS_POOL, 4):
                    step(pool.tensor_tensor(ln.t[:], ln.y[:], ln.y[:], ALU.mult), k + 1)
                    step(pool.tensor_tensor(ln.t[:], ln.t[:], ln.v[:], ALU.mult), k + 2)
                    step(pool.tensor_tensor(ln.t[:], ln.t[:], three_halves[:, 0:ln.tiles], ALU.add), k + 3)
                    step(pool.tensor_tensor(ln.y[:], ln.y[:], ln.t[:], ALU.mult), k + 4)

            def row_ready(n, k):
                if k == 0:
                    has(pool, addressed, n, ADDRESS)
                else:
                    has(pool, w2_in, n)

            def scatter(k, par):
                pool.indirect_dma_start(slot_rows, bass.IndirectOffsetOnAxis(ap=pos[:, k:k + 1].bitcast(U32), axis=0),
                                        pay[:, par, :], None).then_inc(scattered[k], 16)

            def slot(b, u, g, cur, nxt, prv):
                if b is None:
                    pool.memset(ident[:], 0.0).then_inc(consts, 1)
                    pool.memset(causal[:], 0.0).then_inc(consts, 1)
                    pool.memset(pr[:], 0.0).then_inc(consts, 1)
                    pool.memset(three_halves[:], 1.5).then_inc(consts, 1)
                    pool.wait_ge(consts, 6)
                    pool.affine_select(out=ident[:], in_=ident[:], compare_op=ALU.not_equal, fill=1.0, base=0,
                                       pattern=[[-1, P]], channel_multiplier=1).then_inc(consts, 1)
                    pool.wait_ge(consts, 7)
                    pool.affine_select(out=causal[:], in_=causal[:], compare_op=ALU.is_ge, fill=MASKED, base=0,
                                       pattern=[[-1, SEG]], channel_multiplier=1).then_inc(causal_done, 1)
                    pool.wait_ge(causal_done, 1)
                    pool.affine_select(out=causal[SEG:P], in_=causal[SEG:P], compare_op=ALU.is_ge, fill=MASKED, base=0,
                                       pattern=[[-1, SEG]], channel_multiplier=1).then_inc(consts, 1)
                    pool.wait_ge(consts, 8)
                    pool.memset(empty[:], 0.0).then_inc(empty_done, 1)
                    pool.wait_ge(empty_done, 1)
                    pool.memset(empty[:, D:D + 1].bitcast(I32), NO_TOKEN).then_inc(empty_done, 1)
                    pool.iota(filled[:], [[REGION, EXPERTS]], base=0, channel_multiplier=0,
                              allow_small_or_imprecise_dtypes=True).then_inc(rt_made, 1)
                    pool.iota(lowest[:], [[-1, EXPERTS]], base=EXPERTS, channel_multiplier=0,
                              allow_small_or_imprecise_dtypes=True).then_inc(rt_made, 1)
                    pool.iota(pay[:, :, D].bitcast(I32), [[P, 2]], base=-2 * P, channel_multiplier=1).then_inc(rt_made, 1)
                    pool.memset(all_ones[:], 1.0).then_inc(rt_made, 1)
                    pool.memset(before[:], 1.0).then_inc(before_set, 1)
                    pool.wait_ge(before_set, 1)
                    pool.affine_select(out=before[:], in_=before[:], compare_op=ALU.is_gt, fill=0.0, base=0,
                                       pattern=[[1, P]], channel_multiplier=-1).then_inc(rt_made, 1)
                    pool.iota(tile_no[:], [[1, N_TILES], [0, EXPERTS]], base=0, channel_multiplier=0,
                              allow_small_or_imprecise_dtypes=True).then_inc(table_made, 1)
                    pool.iota(tile_start[:], [[P, N_TILES]], base=0, channel_multiplier=0,
                              allow_small_or_imprecise_dtypes=True).then_inc(table_made, 1)
                    pool.iota(region_start[:], [[REGION, EXPERTS]], base=0, channel_multiplier=0,
                              allow_small_or_imprecise_dtypes=True).then_inc(table_made, 1)
                    pool.memset(ones8[:], 1.0).then_inc(table_made, 1)
                if cur:
                    has(pool, mx_done, u)
                    pool.tensor_tensor(sm[:], sm[:], mx[:, :, None].broadcast_to([P, 4, SEG]), ALU.subtract).then_inc(sub_done, 1)
                if prv:
                    has(pool, attm_done[2], u - 1)
                    has(pool, dotb_done, u - 1)
                    pool.tensor_tensor(att[:], att[:], attm[:], ALU.add).then_inc(att_done, 1)
                if cur and g == PAIRS - 4 and not (isinstance(b, int) and b == BATCH - 1):
                    rsqrt(ln1, b + 1)
                if routed_half(b, g) is not None and g % 4 == 1 and cur:
                    rsqrt(ln2, routed_half(b, g))
                if b is not None and not cur:
                    rsqrt(ln2, TILES - 2)
                    for n in (TILES - 3, TILES - 2, TILES - 1):
                        row_ready(n, 0)
                        scatter(0, n % 2)
                        if n < TILES - 1:
                            row_ready(n, 1)
                            scatter(1, n % 2)
                        else:
                            scatter(1, 1 - n % 2)
                if isinstance(u, int) and u == 0:
                    pool.wait_ge(beta_ready, 2)
                if cur:
                    sent = sent_half(b, g) if g % 4 >= 2 else None
                    if sent is not None:
                        row_ready(sent, g % 4 - 2)
                    has(pool, dot_done, u)
                    pool.tensor_tensor(att[:], att[:], beta_rest[:, g, :, None, :].broadcast_to([P, 2, 2, DK]),
                                       ALU.mult).then_inc(dotb_done, 1)
                    if sent is not None:
                        scatter(g % 4 - 2, (g // 4 + 1) % 2)

            run_slots(pool, slot)


def experts(nc, gate_up, down, slots, hi, lo, ident, out):
    RING = 4
    LATE = WX - WG
    assert LATE == INNER
    CHUNKS = EXPERTS // 2
    ctx = ExitStack()
    with ctx:
        def sb(name, shape, dt=F32):
            return ctx.enter_context(nc.sbuf_tensor(name, shape, dt))

        def bank(name):
            return ctx.enter_context(nc.psum_tensor(name, [P, 512], F32))

        def sem(name):
            return ctx.enter_context(nc.semaphore(name))

        late_hi, late_lo = (sb(n, [P, EXPERTS, LATE], F32R) for n in ("late_hi", "late_lo"))

        def gate_up_of(e, half, c):
            if (half, c) == (1, KC - 1):
                return late_hi[:, bass.ds(e, 1)], late_lo[:, bass.ds(e, 1)]
            o = (2 * c + half) * INNER
            return hi[:, bass.ds(e, 1), o:o + INNER], lo[:, bass.ds(e, 1), o:o + INNER]

        late = sb("late", [P, EXPERTS, LATE])
        dn = sb("dn", [P, EXPERTS, IC, D])
        tile_expert, tile_row = slots.tile_expert, slots.tile_row
        PX, PH = bank("PX"), bank("PH")
        PG, PU, PY = ([bank(f"{n}{i}") for i in range(2)] for n in ("PG", "PU", "PY"))

        late_dma = [sem(f"late_dma{i}") for i in range(CHUNKS)]
        late_hi_done, late_lo_done, dn_dma = sem("late_hi_done"), sem("late_lo_done"), sem("dn_dma")

        slot = [sb(f"slot{i}", [P, ROW]) for i in range(RING)]
        xT_hi = [sb(f"exT_hi{i}", [P, KC, P], F32R) for i in range(2)]
        xT_lo = [sb(f"exT_lo{i}", [P, KC, P], F32R) for i in range(2)]
        act_g = [sb(f"act_g{i}", [P, INNER]) for i in range(2)]
        hid = [sb(f"hid{i}", [P, INNER]) for i in range(2)]
        hidT = [sb(f"hidT{i}", [P, IC, P]) for i in range(2)]
        y = [sb(f"y{i}", [P, D]) for i in range(2)]
        row_of = [sb(f"row_of{i}", [P, 1], I32) for i in range(2)]
        zero_i = sb("zero_i", [P, 1], I32)
        indexed, zeroed = sem("m_indexed"), sem("m_zeroed")
        late_of = [slice(2 * c, 2 * c + 2) for c in range(CHUNKS)]
        slot_dma = [sem(f"slot_dma{i}") for i in range(RING)]
        xt, xhi, xlo, gated, upped, silu, hid_done, ht, hidT_done, yt, y_done, added = (sem(n) for n in (
            "m_xt", "m_xhi", "m_xlo", "m_gated", "m_upped", "m_silu", "m_hid", "m_ht", "m_hidT", "m_yt", "m_y", "m_added"))

        def load_late(engine, c):
            engine.dma_start(late[:, late_of[c], :], gate_up[late_of[c], :, WG:WX].rearrange("e p n -> p e n"))\
                  .then_inc(late_dma[c], 16)

        def steps(engine, body):
            rounds = N_TILES // RING - 1
            for q in range(RING):
                body(q, q, 0)
            with engine.Fori(1, rounds) as jj:
                for q in range(RING):
                    body(RING * jj + q, q, jj)
            for j in range(RING * rounds, N_TILES):
                body(j, j % RING, j // RING)

        def loaded(eng, q, jj):
            eng.wait_ge(slot_dma[q % RING], (jj + q // RING + 1) * 16)

        def ends_of(j, q):
            return q % 2, isinstance(j, int) and j == 0, isinstance(j, int) and j == N_TILES - 1

        def has(eng, s, j):
            if isinstance(j, int) and j < 0:
                return
            eng.wait_ge(s, j + 1)

        with nc.Block() as block:
            @block.sync
            def _(sp):
                def load_down(e):
                    if e:
                        sp.wait_ge(dn_dma, 16 * e)
                    sp.dma_start(dn[:, e], down[e]).then_inc(dn_dma, 16)

                def first_row(j):
                    return sp.value_load(tile_row[0:1, bass.ds(j, 1)], min_val=0, max_val=SLOTS - P)

                def load(row, i):
                    sp.dma_start(slot[i][:], slots.rows[bass.ds(row, P), :]).then_inc(slot_dma[i], 16)

                for k in range(2):
                    sp.wait_ge(slots.scattered[k], 16 * TILES)
                sp.wait_ge(slots.pad_dma, 16 * EXPERTS)
                for q in range(RING):
                    load(first_row(q), q)
                    if q == 1:
                        load_late(sp, 0)
                for e in range(2):
                    load_down(e)

                def body(j, q, jj):
                    if isinstance(j, int) and j + RING >= N_TILES:
                        return
                    row = first_row(j + RING)
                    done = j + 1 if isinstance(j, int) else sp.snap(j + 1)
                    sp.wait_ge(xt, done)
                    sp.wait_ge(y_done, done)
                    sp.wait_ge(indexed, done)
                    load(row, q)
                    if isinstance(j, int) and j < RING:
                        for e in ((2,), (3,), (4, 5), (6, 7))[j]:
                            load_down(e)

                steps(sp, body)

            @block.tensor
            def _(pe):
                def turn_x(j, q, jj):
                    loaded(pe, q, jj)
                    has(pe, xlo, j - 1)
                    for c in range(KC):
                        m = pe.transpose(PX[:, c * P:(c + 1) * P], slot[q % RING][:, c * P:(c + 1) * P], ident[:])
                    m.then_inc(xt, 1)

                def body(j, q, jj):
                    i, first, last = ends_of(j, q)
                    if first:
                        turn_x(0, 0, 0)
                    if not last:
                        turn_x(j + 1, q + 1, jj)
                    e = pe.value_load(tile_expert[0:1, bass.ds(j, 1)], min_val=0, max_val=EXPERTS - 1)
                    has(pe, xlo, j)
                    if not first:
                        has(pe, hid_done, j - 2)
                    for half, dst, done in ((0, PG[i], gated), (1, PU[i], upped)):
                        for c in range(KC):
                            if (half, c) == (1, KC - 1) and isinstance(j, int) and j < EXPERTS:
                                pe.wait_ge(late_lo_done, j // 2 + 1)
                            w_hi, w_lo = gate_up_of(e, half, c)
                            pe.matmul(dst[:], xT_hi[i][:, c], w_lo, start=c == 0, stop=False)
                            pe.matmul(dst[:], xT_hi[i][:, c], w_hi, start=False, stop=False)
                            m = pe.matmul(dst[:], xT_lo[i][:, c], w_hi, start=False, stop=c == KC - 1)
                        m.then_inc(done, 1)
                        if half == 0 and not first:
                            turn_hidden(j - 1, 1 - i)
                    if not first:
                        project_down(j - 1, 1 - i)
                    if last:
                        turn_hidden(j, i)
                        project_down(j, i)

                def turn_hidden(j, i):
                    has(pe, hid_done, j)
                    has(pe, hidT_done, j - 1)
                    for c in range(IC):
                        m = pe.transpose(PH[:, c * P:(c + 1) * P], hid[i][:, c * P:(c + 1) * P], ident[:])
                    m.then_inc(ht, 1)

                def project_down(j, i):
                    e = pe.value_load(tile_expert[0:1, bass.ds(j, 1)], min_val=0, max_val=EXPERTS - 1)
                    has(pe, hidT_done, j)
                    pe.wait_ge(dn_dma, (e + 1) * 16)
                    if not (isinstance(j, int) and j < 2):
                        has(pe, y_done, j - 2)
                    for c in range(IC):
                        m = pe.matmul(PY[i][:, 0:D], hidT[i][:, c], dn[:, bass.ds(e, 1), c, :], start=c == 0, stop=c == IC - 1)
                    m.then_inc(yt, 1)

                steps(pe, body)

            @block.scalar
            def _(act):
                def body(j, q, jj):
                    i, first, last = ends_of(j, q)
                    if first:
                        split(0, 0)
                    if not last:
                        split(j + 1, 1 - i)
                    if first:
                        split_late_hi(0)
                        for c in range(1, CHUNKS):
                            load_late(act, c)
                    has(act, gated, j)
                    has(act, hid_done, j - 2)
                    act.activation(act_g[i][:], PG[i][:], ACT.Silu).then_inc(silu, 1)
                    if not first:
                        turned(j - 1, 1 - i)
                    if isinstance(j, int) and j + 1 < CHUNKS:
                        split_late_hi(j + 1)
                    if last:
                        turned(j, i)

                def split(j, i):
                    has(act, xt, j)
                    act.activation(xT_hi[i][:], PX[:, 0:KC * P], ACT.Copy).then_inc(xhi, 1)

                def turned(j, i):
                    has(act, ht, j)
                    act.activation(hidT[i][:], PH[:], ACT.Copy).then_inc(hidT_done, 1)

                def split_late_hi(c):
                    act.wait_ge(late_dma[c], 16)
                    act.activation(late_hi[:, late_of[c]], late[:, late_of[c]], ACT.Copy).then_inc(late_hi_done, 1)

                steps(act, body)

            @block.vector
            def _(dve):
                def body(j, q, jj):
                    i, first, last = ends_of(j, q)
                    if first:
                        split(0, 0)
                    if not last:
                        split(j + 1, 1 - i)
                    if first:
                        split_late_lo(0)
                    has(dve, silu, j)
                    has(dve, upped, j)
                    if not first:
                        has(dve, ht, j - 2)
                    dve.tensor_tensor(hid[i][:], act_g[i][:], PU[i][:], ALU.mult).then_inc(hid_done, 1)
                    if not first:
                        weigh(j - 1, q - 1)
                    if isinstance(j, int) and j + 1 < CHUNKS:
                        split_late_lo(j + 1)
                    if last:
                        weigh(j, q)

                def split(j, i):
                    has(dve, xhi, j)
                    dve.tensor_tensor(xT_lo[i][:], PX[:, 0:KC * P], xT_hi[i][:], ALU.subtract).then_inc(xlo, 1)

                def weigh(j, q):
                    i = q % 2
                    has(dve, yt, j)
                    if not (isinstance(j, int) and j < 2):
                        dve.wait_ge(added, (j - 1) * 16)
                    dve.tensor_scalar(y[i][:], PY[i][:, 0:D], slot[q % RING][:, D + 1:D + 2], None, ALU.mult).then_inc(y_done, 1)

                def split_late_lo(c):
                    dve.wait_ge(late_hi_done, c + 1)
                    dve.tensor_tensor(late_lo[:, late_of[c]], late[:, late_of[c]], late_hi[:, late_of[c]],
                                      ALU.subtract).then_inc(late_lo_done, 1)

                steps(dve, body)

            @block.gpsimd
            def _(pool):
                last_row = pool.to_reg(TILES * P - 1)
                pool.memset(zero_i[:], 0).then_inc(zeroed, 1)
                pool.wait_ge(zeroed, 1)

                def take_index(q, jj):
                    loaded(pool, q, jj)
                    pool.tensor_tensor(row_of[q % 2][:], slot[q % RING][:, D:D + 1].bitcast(I32), zero_i[:], ALU.add).then_inc(indexed, 1)

                def body(j, q, jj):
                    i, first, last = ends_of(j, q)
                    if first:
                        take_index(0, 0)
                    has(pool, indexed, j)
                    has(pool, y_done, j)
                    if not first:
                        pool.wait_ge(added, j * 16)
                    if not last:
                        take_index(q + 1, jj)
                    pool.indirect_dma_start(out, bass.IndirectOffsetOnAxis(ap=row_of[i][:].bitcast(U32), axis=0),
                                            y[i][:], None, bounds_check=last_row, oob_is_err=False,
                                            compute_op=ALU.add).then_inc(added, 16)

                steps(pool, body)
                pool.wait_ge(added, N_TILES * 16)


def program(nc, x_ln, x_res, Wqkv, Wo, betas, gate, gate_up, down, out):
    with ExitStack() as ctx:
        slots = Slots(nc, ctx)
        hi, lo = (ctx.enter_context(nc.sbuf_tensor(n, [P, EXPERTS, WG], F32R)) for n in ("hi", "lo"))
        ident = ctx.enter_context(nc.sbuf_tensor("ident", [P, P], F32))
        attention(nc, x_ln, x_res, Wqkv, Wo, betas, gate, gate_up, out, slots, hi, lo, ident)
        experts(nc, gate_up, down, slots, hi, lo, ident, out.rearrange("n p d -> (n p) d"))


SEGMENTS_IN = [0, 1, 3, 2]
SEGMENTS_OUT = [1, 0, 2, 3]


def kernel(**inputs):
    import concourse.bacc as bacc
    from concourse.bass_utils import run_bass_kernel_spmd

    a = {k: np.asarray(v) for k, v in inputs.items()}
    x = a["L0_attn_x"].reshape(BATCH, NSEG, SEG, D)
    by_pair = [a[f"L0_attn_W{c}"].reshape(KC, P, PAIRS, PW).transpose(2, 1, 0, 3) for c in "qkv"]
    half = HEADS // 2 * 4
    arrays = {
        "x_ln": x[:, SEGMENTS_IN].reshape(BATCH, 2, P, D).transpose(0, 2, 1, 3),
        "x_res": x.reshape(BATCH, NSEG, 2, half, D)[:, SEGMENTS_OUT].transpose(0, 2, 1, 3, 4).reshape(TILES, P, D),
        "Wqkv": np.stack(by_pair, 2).reshape(PAIRS, P, WG),
        "Wo": a["L0_attn_Wo"].reshape(PAIRS, 2, DK, D).transpose(2, 0, 1, 3),
        "betas": a["L0_attn_betas"].reshape(HEADS, DK),
        "gate": a["L0_ffn_gate_weight"].T.reshape(KC, P, EXPERTS).transpose(1, 0, 2),
        "gate_up": a["L0_ffn_gate_up_proj"].reshape(EXPERTS, 2 * INNER, KC, P).transpose(0, 3, 2, 1).reshape(EXPERTS, P, WX),
        "down": a["L0_ffn_down_proj"].reshape(EXPERTS, D, IC, P).transpose(0, 3, 2, 1),
    }
    arrays = {k: np.ascontiguousarray(v) for k, v in arrays.items()}
    nc = bacc.Bacc("TRN2", target_bir_lowering=False, num_devices=1)
    args = [nc.dram_tensor(k, v.shape, mybir.dt.from_np(v.dtype), kind="ExternalInput").ap() for k, v in arrays.items()]
    out = nc.dram_tensor("out", (TILES, P, D), F32, kind="ExternalOutput").ap()
    program(nc, *args, out)
    got = run_bass_kernel_spmd(nc, [arrays], core_ids=[0]).results[0]["out"]
    back = np.argsort(SEGMENTS_OUT)
    got = got.reshape(BATCH, 2, NSEG, half, D).transpose(0, 2, 1, 3, 4)[:, back]
    return np.ascontiguousarray(got.reshape(BATCH, SEQ, D))
```
